# Optimizing a Trainium2 kernel written in Bass

```python
import numpy as np
import jax
import jax.numpy as jnp

def _softmax(x, axis=-1):
    return jax.nn.softmax(x, axis=axis)

def _gelu(x):
    return jax.nn.gelu(x, approximate=True)

def _silu(x):
    return jax.nn.silu(x)

def _sigmoid(x):
    return jax.nn.sigmoid(x)

def _layernorm(x, axis=-1, eps=1e-05):
    m = jnp.mean(x, axis=axis, keepdims=True)
    v = jnp.var(x, axis=axis, keepdims=True)
    return (x - m) / jnp.sqrt(v + eps)

def _scatter_add(tgt, idx, src, axis=0):
    return tgt.at[idx].add(src)

def _segment_sum(src, seg, n):
    return jax.ops.segment_sum(src, seg, n)
kernel_name = 'mk_seq_preln_d1_jaxref_r8_47c918'

def setup_inputs(seed: int=0):
    np.random.seed(seed)
    _w = jnp.asarray

    def _L0_attn_setup():
        import jax, jax.numpy as jnp
        import numpy as np
        import math
        N_HEADS = 16

        def rotate_half(x):
            x1 = x[..., :x.shape[-1] // 2]
            x2 = x[..., x.shape[-1] // 2:]
            return jnp.concatenate([-x2, x1], axis=-1)
        key = jax.random.key(seed)
        ks = jax.random.split(key, 3)
        B, S, D = (2, 256, 256)
        x = jax.random.normal(ks[0], (B, S, D), dtype=jnp.float32)
        w_qkv = jax.random.normal(ks[1], (D, 3 * D), dtype=jnp.float32) * (1.0 / math.sqrt(D))
        b_qkv = jnp.zeros((3 * D,), dtype=jnp.float32)
        w_o = jax.random.normal(ks[2], (D, D), dtype=jnp.float32) * (1.0 / math.sqrt(D))
        b_o = jnp.zeros((D,), dtype=jnp.float32)
        return {'x': x, 'w_qkv': w_qkv, 'b_qkv': b_qkv, 'w_o': w_o, 'b_o': b_o}
    _L0_attn_in = _L0_attn_setup()

    def _L0_ffn_setup():
        import jax, jax.numpy as jnp
        import numpy as np
        B, S, D_IN, D_OUT = (4, 256, 256, 256)
        EPS = 1e-10
        key = jax.random.key(seed)
        kx, kw, kb = jax.random.split(key, 3)
        x = jax.random.normal(kx, (B, S, D_IN), dtype=jnp.float32)
        weight = jax.random.normal(kw, (D_OUT, D_IN), dtype=jnp.float32) * 0.02
        bias = jax.random.normal(kb, (D_OUT,), dtype=jnp.float32) * 0.02
        return {'x': x, 'weight': weight, 'bias': bias}
    _L0_ffn_in = _L0_ffn_setup()
    _d = {'L0_attn_x': _L0_attn_in['x'], 'L0_attn_w_qkv': _L0_attn_in['w_qkv'], 'L0_attn_b_qkv': _L0_attn_in['b_qkv'], 'L0_attn_w_o': _L0_attn_in['w_o'], 'L0_attn_b_o': _L0_attn_in['b_o'], 'L0_ffn_weight': _L0_ffn_in['weight'], 'L0_ffn_bias': _L0_ffn_in['bias']}
    _x0 = _d['L0_attn_x']
    _d['L0_attn_x'] = jax.random.normal(jax.random.fold_in(jax.random.key(seed), 1), (8, 256, 256), dtype=_x0.dtype)
    del _x0
    return _d

def reference(L0_attn_x, L0_attn_w_qkv, L0_attn_b_qkv, L0_attn_w_o, L0_attn_b_o, L0_ffn_weight, L0_ffn_bias):

    def _L0_attn_ref(x, w_qkv, b_qkv, w_o, b_o):
        import jax, jax.numpy as jnp
        import numpy as np
        import math
        N_HEADS = 16

        def rotate_half(x):
            x1 = x[..., :x.shape[-1] // 2]
            x2 = x[..., x.shape[-1] // 2:]
            return jnp.concatenate([-x2, x1], axis=-1)
        B, S, D = x.shape
        H = N_HEADS
        hd = D // H
        qkv = x @ w_qkv + b_qkv
        qkv = qkv.reshape(B, S, H, 3 * hd).transpose(0, 2, 1, 3)
        q, k, v = jnp.split(qkv, 3, axis=-1)
        inv_freq = 1.0 / 10000.0 ** (jnp.arange(0, hd, 2, dtype=jnp.float32) / hd)
        t = jnp.arange(S, dtype=jnp.float32)
        freq = jnp.einsum('s,f->sf', t, inv_freq)
        emb = jnp.concatenate([freq, freq], axis=-1)[None, None]
        sin_cach = jnp.sin(emb)
        cos_cach = jnp.cos(emb)
        cos, sin = (sin_cach, cos_cach)
        q = q * cos + rotate_half(q) * sin
        k = k * cos + rotate_half(k) * sin
        logits = jnp.einsum('bhqd,bhkd->bhqk', q, k) / math.sqrt(hd)
        causal = jnp.tril(jnp.ones((S, S), dtype=bool))[None, None]
        logits = jnp.where(causal, logits, jnp.float32(-9000000000000000.0))
        score = jax.nn.softmax(logits, axis=-1)
        attn = jnp.einsum('bhqk,bhkd->bhqd', score, v)
        attn = attn.transpose(0, 2, 1, 3).reshape(B, S, D)
        return attn @ w_o + b_o

    def _L0_ffn_ref(x, weight, bias):
        import jax, jax.numpy as jnp
        import numpy as np
        B, S, D_IN, D_OUT = (4, 256, 256, 256)
        EPS = 1e-10
        scale = jnp.mean(jnp.abs(weight))
        w_t = jnp.clip(jnp.round(weight / (scale + EPS)), -1.0, 1.0)
        w_ste = weight + jax.lax.stop_gradient(w_t * scale - weight)
        return jnp.einsum('bsi,oi->bso', x, w_ste) + bias
    x = L0_attn_x
    x = x + _L0_attn_ref(_layernorm(x, axis=-1), L0_attn_w_qkv, L0_attn_b_qkv, L0_attn_w_o, L0_attn_b_o)
    x = x + _L0_ffn_ref(_layernorm(x, axis=-1), L0_ffn_weight, L0_ffn_bias)
    return x

_drawn_inputs = setup_inputs


def setup_inputs(seed=0):
    import zlib

    import numpy as np

    out = dict(_drawn_inputs(seed))
    spreads = {'L0_attn_b_qkv': (0.0, 0.1), 'L0_attn_b_o': (0.0, 0.1)}
    factors = {'L0_ffn_bias': 2.938}
    for name, (base, spread) in spreads.items():
        noise = np.random.default_rng([zlib.crc32(name.encode()), seed]).standard_normal(out[name].shape)
        drawn = base * np.exp(spread * noise) if base else spread * noise
        out[name] = jnp.asarray(drawn.astype(out[name].dtype))
    for name, factor in factors.items():
        out[name] = (out[name] * factor).astype(out[name].dtype)
    return out
```

```python
from contextlib import ExitStack

import numpy as np

import concourse.bass as bass
from concourse import mybir

F32 = mybir.dt.float32
F32R = mybir.dt.float32r
BF16 = mybir.dt.bfloat16
ALU = mybir.AluOpType
ACT = mybir.ActivationFunctionType
AX = mybir.AxisListType

P = 128
B, S, D = 8, 256, 256
H, HD = 16, 16
T = S // P
C = D // P
HALF = HD // 2
QK = 2 * D
ROWS = 64
PROD = 3 * HD
PAIRS = H // 2
G = H // 4
VW = 32
FILLS = 3 * G
EPS = 1e-5
TERNARY_EPS = 1e-10
MASKED = -9e15
TAB_COS, TAB_SIN = 0, HD
TAB = HD + 2 * HD
C_TAB, C_ID, C_MASK, C_SEL, C_END = 0, T * TAB, T * TAB + P, T * TAB + 2 * P, T * TAB + 2 * P + 2


class Seq:

    def __init__(self, c, pair=0):
        self.c, self.pair, self.slot = c, pair, c % 2

    def number(self):
        return self.pair * 2 + self.c

    def count(self, per, n):
        least = per * self.c + n
        if isinstance(self.pair, int):
            return least
        assert least > 0
        return self.pair * (2 * per) + least

    def slot_count(self, per, n):
        least = per * (self.c // 2) + n
        if isinstance(self.pair, int):
            return least
        assert least > 0
        return self.pair * per + least


def wait(eng, sem, value):
    if not isinstance(value, int) or value > 0:
        eng.wait_ge(sem, value)


def wait_apart(eng, sem, value, passed):
    wait(eng, sem, value)
    if not isinstance(value, int):
        eng.sem_inc(passed, 1)


def spread(ap, axis, n):
    ap = ap.unsqueeze(axis)
    shape = list(ap.shape)
    shape[axis] = n
    return ap.to_broadcast(shape)


def layer_kernel(nc, x, w_qkv, b_qkv, w_o, b_o, w_f, b_f, consts, out):
    ctx = ExitStack()
    with ctx:
        def sb(name, shape, dt=F32):
            return ctx.enter_context(nc.sbuf_tensor(name, shape, dt))

        def sem(name):
            return ctx.enter_context(nc.semaphore(name))

        const = sb("const", [P, C_END])
        tab = const[:, C_TAB:C_ID].rearrange("p (t n) -> p t n", t=T)
        ident = const[:, C_ID:C_MASK]
        ident_bf = sb("ident_bf", [P, P], BF16)
        mask_bf = sb("mask_bf", [P, 4, P], BF16)
        wqkv = sb("wqkv", [P, C, 3 * D])
        wqk_h = sb("wqk_h", [P, C, QK], F32R)
        wqk_l = sb("wqk_l", [P, C, QK], F32R)
        wv_h = sb("wv_h", [P, C, D], F32R)
        wv_l = sb("wv_l", [P, C, D], F32R)
        wo = sb("wo", [P, C, D])
        wf = sb("wf", [P, C, D])
        wf_up = sb("wf_up", [P, C, D])
        wf_down = sb("wf_down", [P, C, D])
        wf_t = sb("wf_t", [P, C, D])
        wf_abs = sb("wf_abs", [P, 2])
        wf_scale = sb("wf_scale", [P, 4])
        ones = sb("ones", [P, P])
        bias = sb("bias", [2, 5 * D])
        bias_h = sb("bias_h", [2, 5 * D])
        bias_l = sb("bias_l", [2, 5 * D])
        bias_hr = sb("bias_hr", [2, 5 * D], F32R)
        bias_rows = sb("bias_rows", [2, 5 * D], F32R)
        ones_r = sb("ones_r", [2, P], F32R)
        xs = sb("xs", [P, B, T, D])
        stats = sb("stats", [P, T, 6])
        mean_var = sb("mean_var", [P, T, 2])
        rstd = sb("rstd", [P, 2, T])
        minus_half = sb("minus_half", [P, T])
        xn = sb("xn", [P, T, D])
        xn_h = sb("xn_h", [P, C, S], F32R)
        xn_l = sb("xn_l", [P, C, S], F32R)
        rope_c = sb("rope_c", [P, T, QK])
        rope_s = sb("rope_s", [P, T, QK])
        roped = sb("roped", [P, T, H, 2, HD])
        q_parts = sb("q_parts", [P, T, H, ROWS], F32R)
        k_parts = sb("k_parts", [P, T, H, ROWS], F32R)
        q_t = [sb(f"q_t{i}", [P, PAIRS, S], F32R) for i in range(2)]
        k_t = [sb(f"k_t{i}", [P, PAIRS, S], F32R) for i in range(2)]
        v = [sb(f"v{i}", [P, T, H, VW]) for i in range(2)]
        neg_max = sb("neg_max", [P, T, 2, PAIRS])
        max_parts = sb("max_parts", [P, T, 2, H], F32R)
        max_t = sb("max_t", [2 * H, S])
        probs = [sb(f"probs{i}", [P, FILLS // 2, 512]) for i in range(2)]
        o_t = [sb(f"o_t{i}", [P, 2, 512]) for i in range(2)]
        rsum = sb("rsum", [P, T, H])
        attn = sb("attn", [P, T, H, HD])
        attn_t = sb("attn_t", [P, C, S])
        x2 = sb("x2", [P, T, D])
        stats2 = sb("stats2", [P, T, 6])
        mean_var2 = sb("mean_var2", [P, T, 2])
        rstd2 = sb("rstd2", [P, 2, T])
        xn2 = sb("xn2", [P, T, D])
        xn2_t = sb("xn2_t", [P, C, S])
        y = sb("y", [P, B, T, D])

        def bank(name):
            return ctx.enter_context(nc.psum_tensor(name, [P, 512], F32))

        score_ps = [bank(f"score_ps{i}") for i in range(2)]
        scoret_ps = [bank(f"scoret_ps{i}") for i in range(2)]
        pv_ps = bank("pv_ps")
        a0_ps = bank("a0_ps")
        a1_ps = bank("a1_ps")
        c_ps = bank("c_ps")

        consts_in, wqkv_in, w_in, bias_in = (sem(n) for n in ("consts_in", "wqkv_in", "w_in", "bias_in"))
        x_in = [sem(f"x_in{i}") for i in range(3)]
        memsets = sem("memsets")
        dve_passed, pool_passed = sem("dve_passed"), sem("pool_passed")
        masks_made = sem("masks_made")
        wh_made, wl_made = sem("wh_made"), sem("wl_made")
        bias_h_made, bias_made = sem("bias_h_made"), sem("bias_made")
        wf_step, wf_sum_ps, wf_ready, wft_ps, wft_made = (
            sem(n) for n in ("wf_step", "wf_sum_ps", "wf_ready", "wft_ps", "wft_made"))
        stats_step = sem("stats_step")
        var_made = sem("var_made")
        rstd_step, rstd_made = sem("rstd_step"), sem("rstd_made")
        xn_made = sem("xn_made")
        xnt_ps = sem("xnt_ps")
        xnh_made, xnl_made = sem("xnh_made"), sem("xnl_made")
        qk_ps, v_ps = sem("qk_ps"), sem("v_ps")
        rope_mul = sem("rope_mul")
        rope_made = sem("rope_made")
        high_made, low_made = sem("high_made"), sem("low_made")
        v_made = sem("v_made")
        qkt_ps = sem("qkt_ps")
        qkt_even, qkt_odd = sem("qkt_even"), sem("qkt_odd")
        score_done = sem("score_done")
        max_done = sem("max_done")
        maxh_made, max_split = sem("maxh_made"), sem("max_split")
        maxt_ps, maxt_made = sem("maxt_ps"), sem("maxt_made")
        max_rows = [sem(f"max_rows{i}") for i in range(2)]
        scoret_done = sem("scoret_done")
        exp_done = sem("exp_done")
        causal_done = sem("causal_done")
        pv_done = sem("pv_done")
        o_made = sem("o_made")
        ot_ps = sem("ot_ps")
        rsum_made, attn_made = sem("rsum_made"), sem("attn_made")
        attnt_ps, attnt_made = sem("attnt_ps"), sem("attnt_made")
        proj_ps, x2_made = sem("proj_ps"), sem("x2_made")
        stats2_step, var2_made = sem("stats2_step"), sem("var2_made")
        rstd2_step, rstd2_made = sem("rstd2_step"), sem("rstd2_made")
        xn2_made, xn2t_ps, xn2t_made = sem("xn2_made"), sem("xn2t_ps"), sem("xn2t_made")
        ffn_ps, y_made = sem("ffn_ps"), sem("y_made")
        y_out = sem("y_out")

        LOOPS = (B - 2) // 2

        def turns(eng, turn):
            turn(Seq(0), None, None)
            turn(Seq(1), Seq(0), None)
            with eng.Fori(0, LOOPS) as pair:
                for u in range(2):
                    turn(Seq(2 + u, pair), Seq(1 + u, pair), Seq(u, pair))
            turn(None, Seq(B - 1), Seq(B - 2))
            turn(None, None, Seq(B - 1))

        def score_fill(n):
            r, m = n % 2, n // 2
            return (r, 0, range(4 * m, 4 * m + 4), P) if m < 2 else (r, 1, range(2 * m - 4, 2 * m - 2), S)

        def scoret_fill(n):
            r, octet, m = n % 2, n // (FILLS // 2), n % (FILLS // 2) // 2
            first = 4 * octet
            return r, m % 2, (range(first, first + 2), range(first, first + 4), range(first + 2, first + 4))[m]

        GROUP_FILLS = [range(0, 4), range(4, 6), range(6, 10), range(10, FILLS)]

        block = ctx.enter_context(nc.Block())

        @block.sync
        def _(sp):
            sp.dma_start(xs[:, 0], x[0].rearrange("(t p) d -> p t d", p=P)).then_inc(x_in[0], 16)
            sp.dma_start(const[:], consts).then_inc(consts_in, 16)
            sp.dma_start(wqkv[:], w_qkv.rearrange("(c p) n -> p c n", p=P)).then_inc(wqkv_in, 16)
            for part, b, n in ((0, b_qkv, 3 * D), (3 * D, b_o, D), (4 * D, b_f, D)):
                for r in range(2):
                    sp.dma_start(bias[r:r + 1, part:part + n], b.rearrange("(a n) -> a n", a=1)).then_inc(bias_in, 16)
            sp.dma_start(xs[:, 1], x[1].rearrange("(t p) d -> p t d", p=P)).then_inc(x_in[1], 16)
            sp.dma_start(wo[:], w_o.rearrange("(c p) n -> p c n", p=P)).then_inc(w_in, 16)
            sp.dma_start(wf[:], w_f.rearrange("(c p) n -> p c n", p=P)).then_inc(w_in, 16)
            for n in range(2, B):
                sp.dma_start(xs[:, n], x[n].rearrange("(t p) d -> p t d", p=P)).then_inc(x_in[2], 16)

            def turn(a, b, c):
                if b:
                    wait(sp, maxt_made, b.count(1, 1))
                    for part in range(2):
                        for r in range(2):
                            row = ROWS * r + PROD + part
                            src = part * H + r * PAIRS
                            sp.dma_start(q_t[b.slot][row:row + 1, :, :].bitcast(F32),
                                         max_t[src:src + PAIRS, :]).then_inc(max_rows[b.slot], 16)
                if c:
                    wait(sp, y_made, c.count(1, 1))
                    sp.dma_start(out[c.number()].rearrange("(t p) d -> p t d", p=P),
                                 y[:, c.number()]).then_inc(y_out, 16)

            turns(sp, turn)
            sp.wait_ge(y_out, 16 * B)

        @block.gpsimd
        def _(pool):
            nc.gpsimd.memset(minus_half[:], -0.5).then_inc(memsets, 1)
            nc.gpsimd.memset(ones[:], 1.0).then_inc(memsets, 1)
            nc.gpsimd.memset(ones_r[:].bitcast(F32), 1.0).then_inc(memsets, 1)
            for i in range(2):
                nc.gpsimd.memset(v[i][:, :, :, HD:VW], 1.0).then_inc(memsets, 1)
            nc.gpsimd.memset(q_parts[:, :, :, PROD:ROWS].bitcast(F32), 0.0).then_inc(memsets, 1)
            nc.gpsimd.memset(k_parts[:, :, :, PROD:PROD + 2].bitcast(F32), 1.0).then_inc(memsets, 1)
            nc.gpsimd.memset(k_parts[:, :, :, PROD + 2:ROWS].bitcast(F32), 0.0).then_inc(memsets, 1)

            def inverse_deviation(dst, mv, var_sem, step_sem, made_sem, s):
                wait_apart(pool, var_sem, s.count(1, 1), pool_passed)
                nc.gpsimd.tensor_scalar(dst[:, 0], mv[:, :, 1], 1.0, EPS, ALU.mult, ALU.add).then_inc(step_sem, 1)
                wait(pool, step_sem, s.count(1, 1))
                nc.gpsimd.tensor_tensor(dst[:, 1], dst[:, 0], minus_half[:], ALU.pow).then_inc(made_sem, 1)

            def rope_sum(a, t):
                wait(pool, rope_mul, a.count(2, t + 1))
                wait(pool, low_made, a.count(2, t - 1))
                for half in range(2):
                    dst = roped[:, t, :, :, half * HALF:(half + 1) * HALF].rearrange("p h w i -> p (h w) i")
                    cos = rope_c[:, t, half * D:(half + 1) * D].rearrange("p (n i) -> p n i", i=HALF)
                    sin = rope_s[:, t, half * D:(half + 1) * D].rearrange("p (n i) -> p n i", i=HALF)
                    last = nc.gpsimd.tensor_tensor(dst, cos, sin, ALU.add)
                    if half == 0:
                        last.then_inc(rope_made, 1)
                last.then_inc(rope_made, 1)

            def low_parts(a, t):
                wait(pool, high_made, a.count(2, t + 1))
                nc.gpsimd.tensor_tensor(q_parts[:, t, :, HD:2 * HD], roped[:, t, :, 0, :],
                                        q_parts[:, t, :, 0:HD].bitcast(F32), ALU.subtract)
                nc.gpsimd.tensor_tensor(k_parts[:, t, :, 2 * HD:PROD], roped[:, t, :, 1, :],
                                        k_parts[:, t, :, 0:HD].bitcast(F32), ALU.subtract).then_inc(low_made, 1)

            def causal(b, g):
                for n in GROUP_FILLS[g]:
                    wait_apart(pool, exp_done, b.count(FILLS, n + 1), pool_passed)
                    _, _, pairs = scoret_fill(n)
                    blk = probs[g // 2][:, n % 6, :].rearrange("p (h q) -> p h q", h=len(pairs))[:, :, 0:P]
                    nc.gpsimd.affine_select(out=blk, in_=blk, compare_op=ALU.is_ge, fill=0.0, base=0,
                                            pattern=[[0, blk.shape[1]], [1, P]],
                                            channel_multiplier=-1).then_inc(causal_done, 1)

            def turn(a, b, c):
                if a:
                    inverse_deviation(rstd, mean_var, var_made, rstd_step, rstd_made, a)
                    rope_sum(a, 0)
                    rope_sum(a, 1)
                    low_parts(a, 0)
                    low_parts(a, 1)
                if b:
                    causal(b, 0)
                    causal(b, 1)
                    if not c:
                        causal(b, 2)
                        causal(b, 3)
                if c:
                    inverse_deviation(rstd2, mean_var2, var2_made, rstd2_step, rstd2_made, c)
                if b and c:
                    causal(b, 2)
                    causal(b, 3)

            turns(pool, turn)

        @block.scalar
        def _(act):
            act.wait_ge(wqkv_in, 16)
            for c in range(C):
                w = wqkv[:, c, :].rearrange("p (h w s i) -> p h w s i", h=H, w=3, s=2)
                for s in range(2):
                    dst = wqk_h[:, c, s * D:(s + 1) * D].rearrange("p (h w i) -> p h w i", h=H, w=2)
                    nc.scalar.copy(dst, w[:, :, 0:2, s, :]).then_inc(wh_made, 1)
                nc.scalar.copy(wv_h[:, c, :].rearrange("p (h d) -> p h d", h=H),
                               wqkv[:, c, :].rearrange("p (h n) -> p h n", h=H)[:, :, 2 * HD:]).then_inc(wh_made, 1)
            act.wait_ge(bias_in, 16 * 6)
            nc.scalar.copy(bias_hr[:], bias[:]).then_inc(bias_h_made, 1)

            def max_t_copy(b):
                wait(act, maxt_ps, b.count(1, 1))
                if b.c >= 1 or not isinstance(b.pair, int):
                    before = Seq(b.c - 1, b.pair)
                    wait(act, max_rows[before.slot], before.slot_count(64, 64))
                nc.scalar.copy(max_t[:], a1_ps[0:2 * H, 0:S]).then_inc(maxt_made, 1)

            def high_parts(a, t):
                wait(act, rope_made, a.count(4, 2 * t + 2))
                wait(act, qkt_ps, a.count(8, 0))
                nc.scalar.copy(q_parts[:, t].rearrange("p h (r d) -> p h r d", r=4)[:, :, 0:3:2, :],
                               spread(roped[:, t, :, 0, :], 2, 2))
                nc.scalar.copy(k_parts[:, t, :, 0:2 * HD].rearrange("p h (r d) -> p h r d", r=2),
                               spread(roped[:, t, :, 1, :], 2, 2)).then_inc(high_made, 1)

            def qkt_copy(a, n):
                wait(act, qkt_ps, a.count(8, n + 1))
                dst = (q_t if n < 4 else k_t)[a.slot]
                src = a0_ps if n % 2 == 0 else a1_ps
                nc.scalar.copy(dst[:, 2 * (n % 4):2 * (n % 4) + 2, :].rearrange("p u s -> p (u s)"),
                               src[:]).then_inc(qkt_even if n % 2 == 0 else qkt_odd, 1)

            def exps(b, g):
                wait(act, pv_done, b.count(G, g - g % 2 - 2))
                for n in GROUP_FILLS[g]:
                    wait(act, scoret_done, b.count(FILLS, n + 1))
                    nc.scalar.activation(probs[g // 2][:, n % 6, :], scoret_ps[n % 2][:], ACT.Exp).then_inc(exp_done, 1)

            def turn(a, b, c):
                if b:
                    max_t_copy(b)
                if a:
                    wait(act, xnt_ps, a.count(1, 1))
                    wait(act, v_ps, a.count(1, 0))
                    nc.scalar.copy(xn_h[:].rearrange("p c s -> p (c s)"), a0_ps[:]).then_inc(xnh_made, 1)
                if a:
                    wait(act, v_ps, a.count(1, 1))
                    wait(act, pv_done, a.count(G, -G))
                    nc.scalar.copy(v[a.slot][:, :, :, 0:HD].rearrange("p t h d -> p (t h) d"),
                                   a1_ps[:].rearrange("p (n d) -> p n d", d=HD)).then_inc(v_made, 1)
                if b:
                    exps(b, 0)
                if c:
                    wait(act, attnt_ps, c.count(1, 1))
                    nc.scalar.copy(attn_t[:].rearrange("p c s -> p (c s)"), c_ps[:]).then_inc(attnt_made, 1)
                if a:
                    high_parts(a, 0)
                    high_parts(a, 1)
                if b:
                    exps(b, 1)
                if a:
                    wait(act, scoret_done, a.count(FILLS, -FILLS))
                    for n in (0, 1, 3):
                        qkt_copy(a, n)
                if b:
                    exps(b, 2)
                if a:
                    for n in (4, 6, 7):
                        qkt_copy(a, n)
                if c:
                    wait(act, xn2t_ps, c.count(1, 1))
                    nc.scalar.copy(xn2_t[:].rearrange("p c s -> p (c s)"), c_ps[:]).then_inc(xn2t_made, 1)
                if b:
                    exps(b, 3)

            turns(act, turn)

        @block.vector
        def _(dve):
            def normalise(dst, src, mv, rs, made):
                for t in range(T):
                    last = nc.vector.tensor_scalar(dst[:, t], src[t], mv[:, t, 0:1], rs[:, 1, t:t + 1],
                                                   ALU.subtract, ALU.mult)
                last.then_inc(made, 1)

            def statistics(s, st, mv, src, step, made):
                for t in range(T):
                    nc.vector.bn_stats(st[:, t], src[t]).then_inc(step, 1)
                for t in range(T):
                    wait_apart(dve, step, s.count(T, t + 1), dve_passed)
                    last = nc.vector.bn_aggr(mv[:, t], st[:, t])
                last.then_inc(made, 1)

            def x_tiles(a):
                return [xs[:, a.number(), t, :] for t in range(T)]

            def prepare():
                dve.wait_ge(wqkv_in, 16)
                for c in range(C):
                    w = wqkv[:, c, :].rearrange("p (h w s i) -> p h w s i", h=H, w=3, s=2)
                    for s in range(2):
                        dve.wait_ge(wh_made, 3 * c + s + 1)
                        view = dict(h=H, w=2)
                        nc.vector.tensor_tensor(
                            wqk_l[:, c, s * D:(s + 1) * D].rearrange("p (h w i) -> p h w i", **view),
                            w[:, :, 0:2, s, :],
                            wqk_h[:, c, s * D:(s + 1) * D].bitcast(F32).rearrange("p (h w i) -> p h w i", **view),
                            ALU.subtract).then_inc(wl_made, 1)
                    dve.wait_ge(wh_made, 3 * c + 3)
                    nc.vector.tensor_tensor(
                        wv_l[:, c, :].rearrange("p (h d) -> p h d", h=H),
                        wqkv[:, c, :].rearrange("p (h n) -> p h n", h=H)[:, :, 2 * HD:],
                        wv_h[:, c, :].bitcast(F32).rearrange("p (h d) -> p h d", h=H),
                        ALU.subtract).then_inc(wl_made, 1)
                dve.wait_ge(bias_h_made, 1)
                dve.wait_ge(consts_in, 16)
                nc.vector.tensor_tensor(bias_l[:], bias[:], bias_hr[:].bitcast(F32), ALU.subtract).then_inc(bias_made, 1)
                nc.vector.tensor_scalar(bias_h[:], bias_hr[:].bitcast(F32), const[0:2, C_SEL:C_SEL + 1], None,
                                        ALU.mult).then_inc(bias_made, 1)
                dve.wait_ge(bias_made, 2)
                nc.vector.tensor_scalar(bias_l[:], bias_l[:], const[0:2, C_SEL + 1:C_SEL + 2], None,
                                        ALU.mult).then_inc(bias_made, 1)
                dve.wait_ge(bias_made, 3)
                high, low = (z[:, 0:3 * D].rearrange("p (h w s i) -> p h w s i", h=H, w=3, s=2)
                             for z in (bias_h, bias_l))
                for s in range(2):
                    nc.vector.tensor_tensor(bias_rows[:, s * D:(s + 1) * D].rearrange("p (h w i) -> p h w i", h=H, w=2),
                                            high[:, :, 0:2, s, :], low[:, :, 0:2, s, :], ALU.add).then_inc(bias_made, 1)
                high, low = (z[:, 0:3 * D].rearrange("p (h n) -> p h n", h=H)[:, :, 2 * HD:] for z in (bias_h, bias_l))
                nc.vector.tensor_tensor(bias_rows[:, QK:QK + D].rearrange("p (h d) -> p h d", h=H), high, low,
                                        ALU.add).then_inc(bias_made, 1)
                nc.vector.tensor_tensor(bias_rows[:, 3 * D:], bias_h[:, 3 * D:], bias_l[:, 3 * D:],
                                        ALU.add).then_inc(bias_made, 1)
                nc.vector.tensor_copy(ident_bf[:], ident).then_inc(masks_made, 1)
                nc.vector.tensor_copy(mask_bf[:], spread(const[:, C_MASK:C_SEL], 1, 4)).then_inc(masks_made, 1)

            def ternary_sum():
                dve.wait_ge(w_in, 32)
                nc.vector.tensor_reduce(wf_abs[:, 0:1], wf[:], AX.XY, ALU.add,
                                        apply_absolute_value=True).then_inc(wf_step, 1)

            def ternary_weights():
                dve.wait_ge(wf_sum_ps, 1)
                nc.vector.tensor_scalar(wf_scale[:, 0:1], c_ps[:, 0:1], 1.0 / (D * D), None, ALU.mult).then_inc(wf_step, 1)
                dve.wait_ge(wf_step, 2)
                nc.vector.tensor_scalar(wf_scale[:, 1:2], wf_scale[:, 0:1], TERNARY_EPS, 0.5, ALU.add, ALU.mult)
                nc.vector.tensor_scalar(wf_scale[:, 2:3], wf_scale[:, 0:1], TERNARY_EPS, -0.5, ALU.add,
                                        ALU.mult).then_inc(wf_step, 1)
                dve.wait_ge(wf_step, 3)
                nc.vector.tensor_scalar(wf_up[:], wf[:], wf_scale[:, 1:2], wf_scale[:, 0:1], ALU.is_gt, ALU.mult)
                nc.vector.tensor_scalar(wf_down[:], wf[:], wf_scale[:, 2:3], wf_scale[:, 0:1], ALU.is_lt,
                                        ALU.mult).then_inc(wf_step, 1)
                dve.wait_ge(wf_step, 4)
                nc.vector.tensor_tensor(wf_up[:], wf_up[:], wf_down[:], ALU.subtract).then_inc(wf_step, 1)
                dve.wait_ge(wf_step, 5)
                nc.vector.tensor_tensor(wf_down[:], wf_up[:], wf[:], ALU.subtract).then_inc(wf_step, 1)
                dve.wait_ge(wf_step, 6)
                nc.vector.tensor_tensor(wf_up[:], wf[:], wf_down[:], ALU.add).then_inc(wf_ready, 1)
                dve.wait_ge(wft_ps, 1)
                nc.vector.tensor_copy(wf_t[:].rearrange("p c n -> p (c n)"), c_ps[:]).then_inc(wft_made, 1)

            def rope_products(a, t):
                wait(dve, qk_ps, a.count(2, t + 1))
                wait(dve, rope_made, a.count(4, 2 * t - 2))
                src = a1_ps if t == 0 else a0_ps
                n = QK // HD
                nc.vector.tensor_tensor(rope_c[:, t].rearrange("p (n i) -> p n i", i=HD),
                                        src[:].rearrange("p (n i) -> p n i", i=HD),
                                        spread(tab[:, t, TAB_COS:TAB_SIN], 1, n), ALU.mult)
                for half in range(2):
                    other = 1 - half
                    last = nc.vector.tensor_tensor(
                        rope_s[:, t, half * D:(half + 1) * D].rearrange("p (n i) -> p n i", i=HD),
                        src[:, other * D:(other + 1) * D].rearrange("p (n i) -> p n i", i=HD),
                        spread(tab[:, t, TAB_SIN + half * HD:TAB_SIN + (half + 1) * HD], 1, n // 2), ALU.mult)
                last.then_inc(rope_mul, 1)

            def qkt_copy(a, n):
                wait(dve, qkt_ps, a.count(8, n + 1))
                dst = (q_t if n < 4 else k_t)[a.slot]
                src = a0_ps if n % 2 == 0 else a1_ps
                nc.vector.tensor_copy(dst[:, 2 * (n % 4):2 * (n % 4) + 2, :].rearrange("p u s -> p (u s)"),
                                      src[:]).then_inc(qkt_even if n % 2 == 0 else qkt_odd, 1)

            def maxima(a, fills):
                for n in fills:
                    r, t, pairs, keys = score_fill(n)
                    wait(dve, score_done, a.count(FILLS, n + 1))
                    nc.vector.tensor_reduce(neg_max[:, t, r, pairs.start:pairs.stop],
                                            score_ps[r][:].rearrange("p (h k) -> p h k", k=keys),
                                            AX.X, ALU.max, negate=True).then_inc(max_done, 1)

            def split_maxima(b):
                view = neg_max[:].rearrange("p t r u -> p t (r u)")
                dst = max_parts
                wait(dve, max_done, b.count(FILLS, FILLS))
                wait(dve, maxt_ps, b.count(1, 0))
                nc.vector.tensor_copy(dst[:, :, 0], view).then_inc(maxh_made, 1)
                wait(dve, maxh_made, b.count(1, 1))
                nc.vector.tensor_tensor(dst[:, :, 1], view, dst[:, :, 0].bitcast(F32), ALU.subtract).then_inc(max_split, 1)

            def o_copy(b, half):
                wait(dve, pv_done, b.count(G, 2 * half + 2))
                nc.vector.tensor_copy(o_t[b.slot][:, half, :], pv_ps[:]).then_inc(o_made, 1)

            def normalise_attention(c, t):
                wait(dve, ot_ps, c.count(2, t + 1))
                heads = c_ps[:].rearrange("p (h n) -> p h n", h=H)
                nc.vector.reciprocal(rsum[:, t], heads[:, :, HD]).then_inc(rsum_made, 1)
                wait(dve, rsum_made, c.count(2, t + 1))
                nc.vector.tensor_tensor(attn[:, t], heads[:, :, 0:HD], spread(rsum[:, t], 2, HD),
                                        ALU.mult).then_inc(attn_made, 1)

            prepare()
            ternary_sum()

            def turn(a, b, c):
                if b:
                    split_maxima(b)
                if a:
                    if isinstance(a.pair, int):
                        wait(dve, x_in[a.c], 16)
                    else:
                        dve.wait_ge(x_in[2], 16 * (B - 2))
                    statistics(a, stats, mean_var, x_tiles(a), stats_step, var_made)
                if c:
                    normalise_attention(c, 0)
                if a:
                    wait(dve, rstd_made, a.count(1, 1))
                    wait(dve, xnt_ps, a.count(1, 0))
                    normalise(xn, x_tiles(a), mean_var, rstd, xn_made)
                if c:
                    normalise_attention(c, 1)
                if a:
                    wait(dve, xnh_made, a.count(1, 1))
                    wait(dve, v_ps, a.count(1, 0))
                    nc.vector.tensor_tensor(xn_l[:].rearrange("p c s -> p (c s)"), a0_ps[:],
                                            xn_h[:].bitcast(F32).rearrange("p c s -> p (c s)"),
                                            ALU.subtract).then_inc(xnl_made, 1)
                    rope_products(a, 0)
                    rope_products(a, 1)
                if not c and a and not b:
                    ternary_weights()
                if c:
                    wait(dve, proj_ps, c.count(1, 1))
                    nc.vector.tensor_tensor(x2[:].rearrange("p t d -> p (t d)"), c_ps[:],
                                            xs[:, c.number()].rearrange("p t d -> p (t d)"),
                                            ALU.add).then_inc(x2_made, 1)
                    wait(dve, x2_made, c.count(1, 1))
                    statistics(c, stats2, mean_var2, [x2[:, t] for t in range(T)], stats2_step, var2_made)
                if a:
                    qkt_copy(a, 2)
                if b:
                    o_copy(b, 0)
                if a:
                    qkt_copy(a, 5)
                if c:
                    wait(dve, rstd2_made, c.count(1, 1))
                    normalise(xn2, [x2[:, t] for t in range(T)], mean_var2, rstd2, xn2_made)
                if a:
                    maxima(a, range(8))
                if c:
                    wait(dve, ffn_ps, c.count(1, 1))
                    nc.vector.tensor_tensor(y[:, c.number()].rearrange("p t d -> p (t d)"), c_ps[:],
                                            x2[:].rearrange("p t d -> p (t d)"), ALU.add).then_inc(y_made, 1)
                if b:
                    o_copy(b, 1)
                if a:
                    maxima(a, range(8, FILLS))

            turns(dve, turn)

        @block.tensor
        def _(pe):
            mm = nc.tensor.matmul

            def transposed(dst, src, sig, value=1):
                for c in range(C):
                    for t in range(T):
                        last = nc.tensor.transpose(dst[:, c * S + t * P:c * S + (t + 1) * P],
                                                   src[:, t, c * P:(c + 1) * P], ident)
                last.then_inc(sig, value)

            def ternary_scale():
                pe.wait_ge(wf_step, 1)
                pe.wait_ge(memsets, 8)
                mm(c_ps[:, 0:1], ones[:], wf_abs[:, 0:1], start=True, stop=True).then_inc(wf_sum_ps, 1)

            def ternary_transpose():
                pe.wait_ge(wf_ready, 1)
                transposed(c_ps, wf_up, wft_ps)

            def project(a, dst, wh, wl, cols, bias_from, t, sig):
                n = cols.stop - cols.start
                mm(dst[:, cols], ones_r[:], bias_rows[:, bias_from:bias_from + n], start=True, stop=False)
                for c in range(C):
                    toks = slice(t * P, (t + 1) * P)
                    for xpart, wpart in ((xn_h, wh), (xn_h, wl), (xn_l, wh)):
                        last = mm(dst[:, cols], xpart[:, c, toks], wpart[:, c, :], start=False,
                                  stop=c == C - 1 and xpart is xn_l)
                if sig is not None:
                    last.then_inc(sig, 1)

            def qkv(a):
                if isinstance(a.pair, int) and a.c == 0:
                    pe.wait_ge(bias_made, 7)
                    pe.wait_ge(wl_made, 6)
                    pe.wait_ge(memsets, 8)
                wait(pe, xnh_made, a.count(1, 1))
                wait(pe, xnl_made, a.count(1, 1))
                wait(pe, maxt_made, a.count(1, 0))
                wait(pe, qkt_odd, a.count(4, 0))
                project(a, a1_ps, wqk_h, wqk_l, slice(0, QK), 0, 0, qk_ps)
                project(a, a0_ps, wqk_h, wqk_l, slice(0, QK), 0, 1, qk_ps)
                wait(pe, rope_mul, a.count(2, 1))
                project(a, a1_ps, wv_h, wv_l, slice(0, D), QK, 0, None)
                project(a, a1_ps, wv_h, wv_l, slice(D, 2 * D), QK, 1, v_ps)

            def qk_transpose(a, banks):
                for n in banks:
                    if n == 0:
                        wait(pe, low_made, a.count(2, 2))
                        wait(pe, rope_mul, a.count(2, 2))
                    if n == 1:
                        wait(pe, v_made, a.count(1, 1))
                    if n >= 2:
                        wait(pe, qkt_even if n % 2 == 0 else qkt_odd, a.count(4, n // 2))
                    dst = a0_ps if n % 2 == 0 else a1_ps
                    for i in range(2):
                        u = 2 * (n % 4) + i
                        for t in range(T):
                            parts = (q_parts if n < 4 else k_parts)[:, t, 2 * u:2 * u + 2, :]
                            src = parts.bitcast(F32).rearrange("p h n -> p (h n)")
                            last = nc.tensor.transpose(dst[:, i * S + t * P:i * S + (t + 1) * P], src, ident)
                    last.then_inc(qkt_ps, 1)

            def scores(a, fills):
                for n in fills:
                    r, t, pairs, keys = score_fill(n)
                    if n == 0:
                        wait(pe, qkt_even, a.count(4, 4))
                        wait(pe, qkt_odd, a.count(4, 4))
                        if isinstance(a.pair, int) and a.c == 0:
                            pe.wait_ge(masks_made, 2)
                    wait(pe, max_done, a.count(FILLS, n - 1))
                    dst = score_ps[r]
                    diagonal = dst[:].rearrange("p (h k) -> p h k", k=keys)[:, :, keys - P:keys]
                    mm(diagonal, ident_bf[:], mask_bf[:, 0:len(pairs), :], start=True, stop=False,
                       skip_group_check=True)
                    rows = slice(ROWS * r, ROWS * r + PROD)
                    for i, u in enumerate(pairs):
                        last = mm(dst[:, i * keys:(i + 1) * keys], q_t[a.slot][rows, u, t * P:(t + 1) * P],
                                  k_t[a.slot][rows, u, 0:keys], start=False, stop=u == pairs[-1],
                                  skip_group_check=True)
                    last.then_inc(score_done, 1)

            def maxima_transpose(b):
                wait(pe, max_split, b.count(1, 1))
                wait(pe, qkt_odd, b.count(4, 4))
                for t in range(T):
                    last = nc.tensor.transpose(a1_ps[0:2 * H, t * P:(t + 1) * P],
                                               max_parts[:, t].bitcast(F32).rearrange("p w h -> p (w h)"), ident)
                last.then_inc(maxt_ps, 1)

            def scores_t(b, g):
                if g == 0:
                    wait(pe, max_rows[b.slot], b.slot_count(64, 64))
                for n in GROUP_FILLS[g]:
                    wait(pe, exp_done, b.count(FILLS, n - 1))
                    r, t, pairs = scoret_fill(n)
                    width = S - t * P
                    rows = slice(ROWS * r, ROWS * (r + 1))
                    for i, u in enumerate(pairs):
                        last = mm(scoret_ps[r][:, i * width:(i + 1) * width],
                                  k_t[b.slot][rows, u, t * P:(t + 1) * P],
                                  q_t[b.slot][rows, u, t * P:S], start=True, stop=True)
                    last.then_inc(scoret_done, 1)

            def values(b, g):
                wait(pe, causal_done, b.count(FILLS, GROUP_FILLS[g].stop))
                wait(pe, v_made, b.count(1, 1))
                if g % 2 == 0:
                    wait(pe, o_made, b.count(2, g // 2))
                pr, e = probs[g // 2], g % 2
                base = (g % 2) * S
                for t in range(T):
                    for i in range(4):
                        u, r = i // 2, i % 2
                        if t == 0:
                            src = pr[:, 4 * e + r, u * S:(u + 1) * S]
                        else:
                            src = pr[:, 2 + r, (2 * e + u) * P:(2 * e + u + 1) * P]
                        last = mm(pv_ps[VW * i:VW * (i + 1), base + t * P:base + S], v[b.slot][:, t, 4 * g + i, :],
                                  src, start=t == 0, stop=t == 1)
                last.then_inc(pv_done, 1)

            def o_transpose(c):
                wait(pe, o_made, c.count(2, 2))
                for t in range(T):
                    if t == 1:
                        wait(pe, attn_made, c.count(2, 1))
                    for g in range(G):
                        last = nc.tensor.transpose(
                            c_ps[:, g * P:(g + 1) * P],
                            o_t[c.slot][:, g // 2, (g % 2) * S + t * P:(g % 2) * S + (t + 1) * P], ident)
                    last.then_inc(ot_ps, 1)

            def linear(src_t, w, bias_from, sig):
                for t in range(T):
                    cols = slice(t * D, (t + 1) * D)
                    mm(c_ps[:, cols], ones_r[:], bias_rows[:, bias_from:bias_from + D], start=True, stop=False)
                    for c in range(C):
                        last = mm(c_ps[:, cols], src_t[:, c, t * P:(t + 1) * P], w[:, c, :], start=False, stop=c == C - 1)
                last.then_inc(sig, 1)

            pe.wait_ge(consts_in, 16)

            def turn(a, b, c):
                first = a and not b
                if c:
                    o_transpose(c)
                if b:
                    maxima_transpose(b)
                if a:
                    wait(pe, xn_made, a.count(1, 1))
                    wait(pe, qkt_even, a.count(4, 0))
                    transposed(a0_ps, xn, xnt_ps)
                    qkv(a)
                if first:
                    ternary_scale()
                if b:
                    scores_t(b, 0)
                if c:
                    wait(pe, attn_made, c.count(2, 2))
                    transposed(c_ps, attn[:].rearrange("p t h d -> p t (h d)"), attnt_ps)
                if b:
                    scores_t(b, 1)
                    values(b, 0)
                if a:
                    qk_transpose(a, range(0, 4))
                if c:
                    wait(pe, attnt_made, c.count(1, 1))
                    linear(attn_t, wo, 3 * D, proj_ps)
                if b:
                    scores_t(b, 2)
                    values(b, 1)
                if first:
                    ternary_transpose()
                if a:
                    qk_transpose(a, range(4, 8))
                if c:
                    wait(pe, xn2_made, c.count(1, 1))
                    transposed(c_ps, xn2, xn2t_ps)
                if b:
                    scores_t(b, 3)
                if a:
                    scores(a, range(0, 4))
                if b:
                    values(b, 2)
                if a:
                    scores(a, range(4, 8))
                if c:
                    wait(pe, xn2t_made, c.count(1, 1))
                    linear(xn2_t, wf_t, 4 * D, ffn_ps)
                if b:
                    values(b, 3)
                if a:
                    scores(a, range(8, FILLS))

            turns(pe, turn)


def constants():
    inv_freq = (np.float32(1.0) / np.float32(10000.0) ** (np.arange(0, HD, 2, dtype=np.float32) / np.float32(HD)))
    freq = np.arange(S, dtype=np.float32)[:, None] * inv_freq.astype(np.float32)[None, :]
    for_x, for_rotated = np.sin(freq), np.cos(freq)
    scale = np.float32(HD ** -0.5)
    table = np.zeros((P, C_END), np.float32)
    for t in range(T):
        rows = slice(t * P, (t + 1) * P)
        at = C_TAB + t * TAB
        table[:, at:at + HD] = np.concatenate([for_x[rows] * scale, for_x[rows]], 1)
        rotated = np.concatenate([for_rotated[rows] * scale, for_rotated[rows]], 1)
        table[:, at + HD:at + 2 * HD] = -rotated
        table[:, at + 2 * HD:at + 3 * HD] = rotated
    table[:, C_ID:C_MASK] = np.eye(P, dtype=np.float32)
    table[:, C_MASK:C_SEL] = np.where(np.arange(P)[None, :] > np.arange(P)[:, None], np.float32(MASKED), np.float32(0))
    table[0, C_SEL] = 1.0
    table[1, C_SEL + 1] = 1.0
    return table


_INS = ["L0_attn_x", "L0_attn_w_qkv", "L0_attn_b_qkv", "L0_attn_w_o", "L0_attn_b_o", "L0_ffn_weight", "L0_ffn_bias"]


def kernel(**inputs):
    import concourse.bacc as bacc
    from concourse.bass_utils import run_bass_kernel_spmd

    nc = bacc.Bacc("TRN2", target_bir_lowering=False, num_devices=1)
    arrays = {f"in_{name}": np.ascontiguousarray(inputs[name]) for name in _INS}
    arrays["in_consts"] = constants()
    args = [nc.dram_tensor(name, a.shape, mybir.dt.from_np(a.dtype), kind="ExternalInput").ap()
            for name, a in arrays.items()]
    args.append(nc.dram_tensor("out_y", (B, S, D), F32, kind="ExternalOutput").ap())
    layer_kernel(nc, *args)
    r = run_bass_kernel_spmd(nc, [arrays], core_ids=[0])
    return r.results[0]["out_y"]
```

```python
from contextlib import ExitStack

import numpy as np

import concourse.bass as bass
from concourse import mybir

F32 = mybir.dt.float32
F32R = mybir.dt.float32r
BF16 = mybir.dt.bfloat16
ALU = mybir.AluOpType
ACT = mybir.ActivationFunctionType
AX = mybir.AxisListType

P = 128
B, S, D = 8, 256, 256
H, HD = 16, 16
T = S // P
C = D // P
HALF = HD // 2
QK = 2 * D
ROWS = 64
PROD = 3 * HD
PAIRS = H // 2
G = H // 4
VW = 32
FILLS = 3 * G
EPS = 1e-5
TERNARY_EPS = 1e-10
MASKED = -9e15
TAB_COS, TAB_SIN = 0, HD
TAB = HD + 2 * HD
C_TAB, C_ID, C_MASK, C_SEL, C_END = 0, T * TAB, T * TAB + P, T * TAB + 2 * P, T * TAB + 2 * P + 2


def do(seq, step, *args):
    if seq:
        step(seq, *args)


def first(seq):
    return seq if seq and isinstance(seq.pair, int) and seq.c == 0 else None


class Seq:

    def __init__(self, c, pair=0):
        self.c, self.pair, self.slot = c, pair, c % 2

    def number(self):
        return self.pair * 2 + self.c

    def count(self, per, n):
        least = per * self.c + n
        if isinstance(self.pair, int):
            return least
        assert least > 0
        return self.pair * (2 * per) + least

    def slot_count(self, per, n):
        least = per * (self.c // 2) + n
        if isinstance(self.pair, int):
            return least
        assert least > 0
        return self.pair * per + least


def wait(eng, sem, value):
    if not isinstance(value, int) or value > 0:
        eng.wait_ge(sem, value)


def wait_apart(eng, sem, value, passed):
    wait(eng, sem, value)
    if not isinstance(value, int):
        eng.sem_inc(passed, 1)


def spread(ap, axis, n):
    ap = ap.unsqueeze(axis)
    shape = list(ap.shape)
    shape[axis] = n
    return ap.to_broadcast(shape)


def layer_kernel(nc, x, w_qkv, b_qkv, w_o, b_o, w_f, b_f, consts, out):
    ctx = ExitStack()
    with ctx:
        def sb(name, shape, dt=F32):
            return ctx.enter_context(nc.sbuf_tensor(name, shape, dt))

        def sem(name):
            return ctx.enter_context(nc.semaphore(name))

        const = sb("const", [P, C_END])
        tab = const[:, C_TAB:C_ID].rearrange("p (t n) -> p t n", t=T)
        ident = const[:, C_ID:C_MASK]
        ident_bf = sb("ident_bf", [P, P], BF16)
        ident_r = sb("ident_r", [P, P], F32R)
        mask_bf = sb("mask_bf", [P, 4, P], BF16)
        wqkv = sb("wqkv", [P, C, 3 * D])
        wqk_h = sb("wqk_h", [P, C, QK], F32R)
        wqk_l = sb("wqk_l", [P, C, QK], F32R)
        wv_h = sb("wv_h", [P, C, D], F32R)
        wv_l = sb("wv_l", [P, C, D], F32R)
        wo = sb("wo", [P, C, D])
        wf = sb("wf", [P, C, D])
        wf_up = sb("wf_up", [P, C, D])
        wf_down = sb("wf_down", [P, C, D])
        wf_t = sb("wf_t", [P, C, D])
        wf_abs = sb("wf_abs", [P, 2])
        wf_scale = sb("wf_scale", [P, 4])
        ones = sb("ones", [P, P])
        bias = sb("bias", [2, 3 * D])
        bias_h = sb("bias_h", [2, 3 * D])
        bias_l = sb("bias_l", [2, 3 * D])
        bias_hr = sb("bias_hr", [2, 3 * D], F32R)
        bias_rows = sb("bias_rows", [2, 3 * D], F32R)
        linear_bias = sb("linear_bias", [P, 2, D])
        ones_r = sb("ones_r", [2, P], F32R)
        xs = sb("xs", [P, B + 1, T, D])
        stats = sb("stats", [P, T, 6])
        mean_var = sb("mean_var", [P, T, 2])
        rstd = sb("rstd", [P, 2, T])
        minus_half = sb("minus_half", [P, T])
        xn = sb("xn", [P, T, D])
        xn_h = sb("xn_h", [P, C, S], F32R)
        xn_l = sb("xn_l", [P, C, S], F32R)
        rope_c = sb("rope_c", [P, T, QK])
        rope_s = sb("rope_s", [P, T, QK])
        roped = sb("roped", [P, T, H, 2, HD])
        q_parts = sb("q_parts", [P, T, H, ROWS], F32R)
        k_parts = sb("k_parts", [P, T, H, ROWS], F32R)
        q_t = [sb(f"q_t{i}", [P, PAIRS, S], F32R) for i in range(2)]
        k_t = [sb(f"k_t{i}", [P, PAIRS, S], F32R) for i in range(2)]
        v = [sb(f"v{i}", [P, T, H, VW]) for i in range(2)]
        neg_max = sb("neg_max", [P, T, 2, PAIRS])
        max_parts = sb("max_parts", [P, T, 2, H], F32R)
        max_t = sb("max_t", [2 * H, S])
        probs = [sb(f"probs{i}", [P, FILLS // 2, 512]) for i in range(2)]
        o_t = [sb(f"o_t{i}", [P, 2, 512]) for i in range(2)]
        rsum = sb("rsum", [P, T, H])
        attn = sb("attn", [P, T, H, HD])
        attn_t = sb("attn_t", [P, C, S])
        x_bias = sb("x_bias", [P, T, D])
        x2 = sb("x2", [P, T, D])
        x2_bias = sb("x2_bias", [P, T, D])
        stats2 = sb("stats2", [P, T, 6])
        mean_var2 = sb("mean_var2", [P, T, 2])
        rstd2 = sb("rstd2", [P, 2, T])
        xn2 = sb("xn2", [P, T, D])
        xn2_t = sb("xn2_t", [P, C, S])

        def bank(name):
            return ctx.enter_context(nc.psum_tensor(name, [P, 512], F32))

        score_ps = [bank(f"score_ps{i}") for i in range(2)]
        scoret_ps = [bank(f"scoret_ps{i}") for i in range(2)]
        pv_ps = bank("pv_ps")
        a0_ps = bank("a0_ps")
        a1_ps = bank("a1_ps")
        c_ps = bank("c_ps")

        consts_in, w_in = sem("consts_in"), sem("w_in")
        wqkv_in = [sem(f"wqkv_in{c}") for c in range(C)]
        bias_in, linear_bias_in = sem("bias_in"), sem("linear_bias_in")
        x_in = [sem(f"x_in{i}") for i in range(3)]
        memsets = sem("memsets")
        dve_passed, pool_passed = sem("dve_passed"), sem("pool_passed")
        masks_made = sem("masks_made")
        wh_made, wl_made = sem("wh_made"), sem("wl_made")
        wvh_made, wvl_made = sem("wvh_made"), sem("wvl_made")
        bias_h_made, bias_made = sem("bias_h_made"), sem("bias_made")
        wf_step, wf_sum_ps, wf_ready, wft_ps = (
            sem(n) for n in ("wf_step", "wf_sum_ps", "wf_ready", "wft_ps"))
        stats_step = sem("stats_step")
        var_made = sem("var_made")
        rstd_step, rstd_made = sem("rstd_step"), sem("rstd_made")
        xn_made = sem("xn_made")
        xnt_ps = sem("xnt_ps")
        xnh_made, xnl_made = sem("xnh_made"), sem("xnl_made")
        qk_ps, v_ps = sem("qk_ps"), sem("v_ps")
        rope_mul = sem("rope_mul")
        rope_made = [sem(f"rope_made{t}") for t in range(T)]
        high_made = sem("high_made")
        low_made = [sem(f"low_made{t}") for t in range(T)]
        v_made = sem("v_made")
        qkt_ps = sem("qkt_ps")
        qkt_act, qkt_dve = sem("qkt_act"), sem("qkt_dve")
        score_done = sem("score_done")
        max_done = sem("max_done")
        maxh_made, max_split = sem("maxh_made"), sem("max_split")
        maxt_ps, maxt_made = sem("maxt_ps"), sem("maxt_made")
        max_rows = [sem(f"max_rows{i}") for i in range(2)]
        scoret_done = sem("scoret_done")
        exp_done = sem("exp_done")
        causal_done = sem("causal_done")
        pv_done = sem("pv_done")
        o_made = [sem(f"o_made{i}") for i in range(2)]
        ot_ps = sem("ot_ps")
        rsum_made, attn_made = sem("rsum_made"), sem("attn_made")
        attnt_ps, attnt_made = sem("attnt_ps"), sem("attnt_made")
        x_bias_made, x2_bias_made = sem("x_bias_made"), sem("x2_bias_made")
        proj_ps, x2_made = sem("proj_ps"), sem("x2_made")
        stats2_step, var2_made = sem("stats2_step"), sem("var2_made")
        rstd2_step, rstd2_made = sem("rstd2_step"), sem("rstd2_made")
        xn2_made, xn2t_ps, xn2t_made = sem("xn2_made"), sem("xn2t_ps"), sem("xn2t_made")
        ffn_ps = sem("ffn_ps")
        y_made = sem("y_made")
        y_out = sem("y_out")

        LOOPS = (B - 2) // 2

        def turns(eng, turn):
            turn(Seq(0), None, None, None)
            turn(Seq(1), Seq(0), None, None)
            turn(Seq(2), Seq(1), Seq(0), None)
            with eng.Fori(0, LOOPS) as pair:
                for u in range(2):
                    turn(Seq(3 + u, pair), Seq(2 + u, pair), Seq(1 + u, pair), Seq(u, pair))
            turn(None, None, Seq(B - 1), Seq(B - 2))
            turn(None, None, None, Seq(B - 1))

        def score_fill(n):
            r, m = n % 2, n // 2
            return (r, 0, range(4 * m, 4 * m + 4), P) if m < 2 else (r, 1, range(2 * m - 4, 2 * m - 2), S)

        def scoret_fill(n):
            r, octet, m = n % 2, n // (FILLS // 2), n % (FILLS // 2) // 2
            first = 4 * octet
            return r, m % 2, (range(first, first + 2), range(first, first + 4), range(first + 2, first + 4))[m]

        GROUP_FILLS = (4, 6, 10, FILLS)

        qkt_banks = [a0_ps, a1_ps, *score_ps]
        QKT_ACT = (0, 2, 3, 4, 6, 7)
        QKT_DVE = (1, 5)

        ot_banks = [c_ps, pv_ps]

        def wait_qkt_evacuated(eng, s, n):
            copied, mine = (qkt_act, QKT_ACT) if n in QKT_ACT else (qkt_dve, QKT_DVE)
            wait(eng, copied, s.count(len(mine), mine.index(n) + 1))

        def wait_qkt_of_last(eng, s, n):
            copied, mine = (qkt_act, QKT_ACT) if n in QKT_ACT else (qkt_dve, QKT_DVE)
            wait(eng, copied, s.count(len(mine), mine.index(n) + 1 - len(mine)))

        def rope_sum(a, eng, t):
            wait(eng, rope_mul, a.count(2, t + 1))
            wait(eng, low_made[t], a.count(1, 0))
            for half in range(2):
                dst = roped[:, t, :, :, half * HALF:(half + 1) * HALF].rearrange("p h w i -> p (h w) i")
                cos = rope_c[:, t, half * D:(half + 1) * D].rearrange("p (n i) -> p n i", i=HALF)
                sin = rope_s[:, t, half * D:(half + 1) * D].rearrange("p (n i) -> p n i", i=HALF)
                last = eng.tensor_tensor(dst, cos, sin, ALU.add)
            last.then_inc(rope_made[t], 1)

        def low_parts(a, eng, t):
            wait(eng, high_made, a.count(2, t + 1))
            eng.tensor_tensor(q_parts[:, t, :, HD:2 * HD], roped[:, t, :, 0, :],
                              q_parts[:, t, :, 0:HD].bitcast(F32), ALU.subtract)
            eng.tensor_tensor(k_parts[:, t, :, 2 * HD:PROD], roped[:, t, :, 1, :],
                              k_parts[:, t, :, 0:HD].bitcast(F32), ALU.subtract).then_inc(low_made[t], 1)

        block = ctx.enter_context(nc.Block())

        @block.sync
        def _(sp):
            sp.dma_start(xs[:, 0], x[0].rearrange("(t p) d -> p t d", p=P)).then_inc(x_in[0], 16)
            sp.dma_start(bias[:], b_qkv.rearrange("(a n) -> a n", a=1).to_broadcast([2, 3 * D])).then_inc(bias_in, 16)
            sp.dma_start(const[:], consts).then_inc(consts_in, 16)
            sp.dma_start(xs[:, 1], x[1].rearrange("(t p) d -> p t d", p=P)).then_inc(x_in[1], 16)
            sp.dma_start(wo[:], w_o.rearrange("(c p) n -> p c n", p=P)).then_inc(w_in, 16)
            sp.dma_start(wf[:], w_f.rearrange("(c p) n -> p c n", p=P)).then_inc(w_in, 16)
            for i, b in enumerate((b_o, b_f)):
                sp.dma_start(linear_bias[:, i, :],
                             b.rearrange("(a n) -> a n", a=1).to_broadcast([P, D])).then_inc(linear_bias_in, 16)
            for n in range(2, B):
                sp.dma_start(xs[:, n], x[n].rearrange("(t p) d -> p t d", p=P)).then_inc(x_in[2], 16)

            def move_maxima(b):
                wait(sp, maxt_made, b.count(1, 1))
                for part in range(2):
                    for r in range(2):
                        row = ROWS * r + PROD + part
                        src = part * H + r * PAIRS
                        sp.dma_start(q_t[b.slot][row:row + 1, :, :].bitcast(F32),
                                     max_t[src:src + PAIRS, :]).then_inc(max_rows[b.slot], 16)

            def store(c):
                wait(sp, y_made, c.count(1, 2))
                sp.dma_start(out[c.number()].rearrange("(t p) d -> p t d", p=P),
                             xs[:, c.number()]).then_inc(y_out, 16)

            def turn(z, a, b, c):
                do(b, move_maxima)
                do(c, store)

            turns(sp, turn)
            sp.wait_ge(y_out, 16 * B)

        @block.gpsimd
        def _(pool):
            nc.gpsimd.memset(minus_half[:], -0.5).then_inc(memsets, 1)

            def fill_constants(_):
                nc.gpsimd.memset(xs[:, B], 0.0).then_inc(memsets, 1)
                nc.gpsimd.memset(ones[:], 1.0).then_inc(memsets, 1)
                nc.gpsimd.memset(ones_r[:].bitcast(F32), 1.0).then_inc(memsets, 1)
                for i in range(2):
                    nc.gpsimd.memset(v[i][:, :, :, HD:VW], 1.0).then_inc(memsets, 1)
                nc.gpsimd.memset(q_parts[:, :, :, PROD:ROWS].bitcast(F32), 0.0).then_inc(memsets, 1)
                nc.gpsimd.memset(k_parts[:, :, :, PROD:PROD + 2].bitcast(F32), 1.0).then_inc(memsets, 1)
                nc.gpsimd.memset(k_parts[:, :, :, PROD + 2:ROWS].bitcast(F32), 0.0).then_inc(memsets, 1)

            def inverse_deviation(dst, mv, var_sem, step_sem, made_sem, s):
                wait_apart(pool, var_sem, s.count(1, 1), pool_passed)
                nc.gpsimd.tensor_scalar(dst[:, 0], mv[:, :, 1], 1.0, EPS, ALU.mult, ALU.add).then_inc(step_sem, 1)
                wait(pool, step_sem, s.count(1, 1))
                nc.gpsimd.tensor_tensor(dst[:, 1], dst[:, 0], minus_half[:], ALU.pow).then_inc(made_sem, 1)

            def causal(b, m):
                for n in (2 * m, 2 * m + 1):
                    wait_apart(pool, exp_done, b.count(FILLS, n + 1), pool_passed)
                    _, _, pairs = scoret_fill(n)
                    blk = probs[n // 6][:, n % 6, :].rearrange("p (h q) -> p h q", h=len(pairs))[:, :, 0:P]
                    nc.gpsimd.affine_select(out=blk, in_=blk, compare_op=ALU.is_ge, fill=0.0, base=0,
                                            pattern=[[0, blk.shape[1]], [1, P]],
                                            channel_multiplier=-1).then_inc(causal_done, 1)

            def add_bias(c):
                if first(c):
                    pool.wait_ge(linear_bias_in, 32)
                nc.gpsimd.tensor_tensor(x_bias[:], xs[:, c.number()], spread(linear_bias[:, 0], 1, T),
                                        ALU.add).then_inc(x_bias_made, 1)

            def add_bias2(c):
                wait(pool, x2_made, c.count(1, 1))
                nc.gpsimd.tensor_tensor(x2_bias[:], x2[:], spread(linear_bias[:, 1], 1, T),
                                        ALU.add).then_inc(x2_bias_made, 1)

            def deviation(z):
                inverse_deviation(rstd, mean_var, var_made, rstd_step, rstd_made, z)

            def deviation2(c):
                inverse_deviation(rstd2, mean_var2, var2_made, rstd2_step, rstd2_made, c)

            def turn(z, a, b, c):
                do(c, causal, 5)
                do(a, rope_sum, pool, 0)
                do(z, deviation)
                do(a, low_parts, pool, 0)
                do(first(z), fill_constants)
                do(c, deviation2)
                do(b, causal, 0)
                do(c, add_bias2)
                do(b, causal, 1)
                do(b, causal, 2)
                do(b, add_bias)
                do(b, causal, 3)
                do(b, causal, 4)

            turns(pool, turn)

        @block.scalar
        def _(act):
            for c in range(C):
                act.dma_start(wqkv[:, c, :], w_qkv[c * P:(c + 1) * P, :]).then_inc(wqkv_in[c], 16)

            def high_weights(_, c):
                act.wait_ge(wqkv_in[c], 16)
                w = wqkv[:, c, :].rearrange("p (h w s i) -> p h w s i", h=H, w=3, s=2)
                for s in range(2):
                    dst = wqk_h[:, c, s * D:(s + 1) * D].rearrange("p (h w i) -> p h w i", h=H, w=2)
                    nc.scalar.copy(dst, w[:, :, 0:2, s, :]).then_inc(wh_made, 1)

            def high_value_weights(_):
                for c in range(C):
                    nc.scalar.copy(wv_h[:, c, :].rearrange("p (h d) -> p h d", h=H),
                                   wqkv[:, c, :].rearrange("p (h n) -> p h n", h=H)[:, :, 2 * HD:]).then_inc(wvh_made, 1)

            def high_bias(_):
                act.wait_ge(bias_in, 16)
                nc.scalar.copy(bias_hr[:], bias[:]).then_inc(bias_h_made, 1)

            def max_t_copy(b):
                wait(act, maxt_ps, b.count(1, 1))
                if b.c >= 1 or not isinstance(b.pair, int):
                    before = Seq(b.c - 1, b.pair)
                    wait(act, max_rows[before.slot], before.slot_count(64, 64))
                nc.scalar.copy(max_t[:], pv_ps[0:2 * H, 0:S]).then_inc(maxt_made, 1)

            def high_parts(a, t):
                wait(act, rope_made[t], a.count(1, 1))
                wait(act, qkt_ps, a.count(8, 0))
                nc.scalar.copy(q_parts[:, t].rearrange("p h (r d) -> p h r d", r=4)[:, :, 0:3:2, :],
                               spread(roped[:, t, :, 0, :], 2, 2))
                nc.scalar.copy(k_parts[:, t, :, 0:2 * HD].rearrange("p h (r d) -> p h r d", r=2),
                               spread(roped[:, t, :, 1, :], 2, 2)).then_inc(high_made, 1)

            def qkt_copy(a, n):
                wait(act, qkt_ps, a.count(8, n + 1))
                wait(act, scoret_done, a.count(FILLS, -FILLS))
                dst = (q_t if n < 4 else k_t)[a.slot]
                nc.scalar.copy(dst[:, 2 * (n % 4):2 * (n % 4) + 2, :].rearrange("p u s -> p (u s)"),
                               qkt_banks[n % 4][:]).then_inc(qkt_act, 1)

            def exps(b, m):
                if m % 3 == 0:
                    wait(act, pv_done, b.count(G, 2 * (m // 3) - 2))
                for n in (2 * m, 2 * m + 1):
                    wait(act, scoret_done, b.count(FILLS, n + 1))
                    nc.scalar.activation(probs[n // 6][:, n % 6, :], scoret_ps[n % 2][:], ACT.Exp).then_inc(exp_done, 1)

            def xn_high(a):
                wait(act, xnt_ps, a.count(1, 1))
                wait(act, v_ps, a.count(1, 0))
                nc.scalar.copy(xn_h[:].rearrange("p c s -> p (c s)"), a0_ps[:]).then_inc(xnh_made, 1)

            def attn_t_copy(c):
                wait(act, attnt_ps, c.count(1, 1))
                nc.scalar.copy(attn_t[:].rearrange("p c s -> p (c s)"), c_ps[:]).then_inc(attnt_made, 1)

            def v_copy(a):
                wait(act, v_ps, a.count(1, 1))
                wait(act, pv_done, a.count(G, -G))
                nc.scalar.copy(v[a.slot][:, :, :, 0:HD].rearrange("p t h d -> p (t h) d"),
                               a1_ps[:].rearrange("p (n d) -> p n d", d=HD)).then_inc(v_made, 1)

            def xn2_t_copy(c):
                wait(act, xn2t_ps, c.count(1, 1))
                nc.scalar.copy(xn2_t[:].rearrange("p c s -> p (c s)"), c_ps[:]).then_inc(xn2t_made, 1)

            def o_copy(c):
                wait(act, pv_done, c.count(G, G))
                nc.scalar.copy(o_t[c.slot][:, 1, :], pv_ps[:]).then_inc(o_made[1], 1)

            def turn(z, a, b, c):
                do(c, exps, 5)
                do(first(z), high_weights, 0)
                do(c, o_copy)
                do(first(z), high_weights, 1)
                do(c, attn_t_copy)
                do(b, max_t_copy)
                do(first(a), high_bias)
                do(a, high_parts, 0)
                do(a, high_parts, 1)
                do(a, v_copy)
                do(a, qkt_copy, 0)
                do(a, qkt_copy, 2)
                do(a, qkt_copy, 3)
                do(b, exps, 0)
                do(a, qkt_copy, 4)
                do(b, exps, 1)
                do(c, xn2_t_copy)
                do(a, qkt_copy, 6)
                do(first(z), high_value_weights)
                do(a, qkt_copy, 7)
                do(b, exps, 2)
                do(z, xn_high)
                do(b, exps, 3)
                do(b, exps, 4)

            turns(act, turn)

        @block.vector
        def _(dve):
            def normalise(dst, src, mv, rs, made):
                for t in range(T):
                    last = nc.vector.tensor_scalar(dst[:, t], src[t], mv[:, t, 0:1], rs[:, 1, t:t + 1],
                                                   ALU.subtract, ALU.mult)
                last.then_inc(made, 1)

            def statistics(s, st, mv, src, step, made):
                for t in range(T):
                    nc.vector.bn_stats(st[:, t], src[t]).then_inc(step, 1)
                for t in range(T):
                    wait_apart(dve, step, s.count(T, t + 1), dve_passed)
                    last = nc.vector.bn_aggr(mv[:, t], st[:, t])
                last.then_inc(made, 1)

            def x_tiles(a):
                return [xs[:, a.number(), t, :] for t in range(T)]

            def low_weights(_, c):
                w = wqkv[:, c, :].rearrange("p (h w s i) -> p h w s i", h=H, w=3, s=2)
                for s in range(2):
                    dve.wait_ge(wh_made, 2 * c + s + 1)
                    view = dict(h=H, w=2)
                    nc.vector.tensor_tensor(
                        wqk_l[:, c, s * D:(s + 1) * D].rearrange("p (h w i) -> p h w i", **view),
                        w[:, :, 0:2, s, :],
                        wqk_h[:, c, s * D:(s + 1) * D].bitcast(F32).rearrange("p (h w i) -> p h w i", **view),
                        ALU.subtract).then_inc(wl_made, 1)

            def low_value_weights(_):
                for c in range(C):
                    dve.wait_ge(wvh_made, c + 1)
                    nc.vector.tensor_tensor(
                        wv_l[:, c, :].rearrange("p (h d) -> p h d", h=H),
                        wqkv[:, c, :].rearrange("p (h n) -> p h n", h=H)[:, :, 2 * HD:],
                        wv_h[:, c, :].bitcast(F32).rearrange("p (h d) -> p h d", h=H),
                        ALU.subtract).then_inc(wvl_made, 1)

            def bias_parts(_):
                dve.wait_ge(bias_h_made, 1)
                dve.wait_ge(consts_in, 16)
                nc.vector.tensor_tensor(bias_l[:], bias[:], bias_hr[:].bitcast(F32), ALU.subtract).then_inc(bias_made, 1)
                nc.vector.tensor_scalar(bias_h[:], bias_hr[:].bitcast(F32), const[0:2, C_SEL:C_SEL + 1], None,
                                        ALU.mult).then_inc(bias_made, 1)
                dve.wait_ge(bias_made, 2)
                nc.vector.tensor_scalar(bias_l[:], bias_l[:], const[0:2, C_SEL + 1:C_SEL + 2], None,
                                        ALU.mult).then_inc(bias_made, 1)
                dve.wait_ge(bias_made, 3)
                high, low = (z[:].rearrange("p (h w s i) -> p h w s i", h=H, w=3, s=2) for z in (bias_h, bias_l))
                for s in range(2):
                    nc.vector.tensor_tensor(bias_rows[:, s * D:(s + 1) * D].rearrange("p (h w i) -> p h w i", h=H, w=2),
                                            high[:, :, 0:2, s, :], low[:, :, 0:2, s, :], ALU.add).then_inc(bias_made, 1)
                high, low = (z[:].rearrange("p (h n) -> p h n", h=H)[:, :, 2 * HD:] for z in (bias_h, bias_l))
                nc.vector.tensor_tensor(bias_rows[:, QK:QK + D].rearrange("p (h d) -> p h d", h=H), high, low,
                                        ALU.add).then_inc(bias_made, 1)

            def masks(_):
                dve.wait_ge(consts_in, 16)
                nc.vector.tensor_copy(ident_bf[:], ident).then_inc(masks_made, 1)
                nc.vector.tensor_copy(ident_r[:], ident).then_inc(masks_made, 1)
                nc.vector.tensor_copy(mask_bf[:], spread(const[:, C_MASK:C_SEL], 1, 4)).then_inc(masks_made, 1)

            def ternary_sum(_):
                dve.wait_ge(w_in, 32)
                nc.vector.tensor_reduce(wf_abs[:, 0:1], wf[:], AX.XY, ALU.add,
                                        apply_absolute_value=True).then_inc(wf_step, 1)

            def ternary_weights(_):
                dve.wait_ge(wf_sum_ps, 1)
                nc.vector.tensor_scalar(wf_scale[:, 0:1], c_ps[:, 0:1], 1.0 / (D * D), None, ALU.mult).then_inc(wf_step, 1)
                dve.wait_ge(wf_step, 2)
                nc.vector.tensor_scalar(wf_scale[:, 1:2], wf_scale[:, 0:1], TERNARY_EPS, 0.5, ALU.add, ALU.mult)
                nc.vector.tensor_scalar(wf_scale[:, 2:3], wf_scale[:, 0:1], TERNARY_EPS, -0.5, ALU.add,
                                        ALU.mult).then_inc(wf_step, 1)
                dve.wait_ge(wf_step, 3)
                nc.vector.tensor_scalar(wf_up[:], wf[:], wf_scale[:, 1:2], wf_scale[:, 0:1], ALU.is_gt, ALU.mult)
                nc.vector.tensor_scalar(wf_down[:], wf[:], wf_scale[:, 2:3], wf_scale[:, 0:1], ALU.is_lt,
                                        ALU.mult).then_inc(wf_step, 1)
                dve.wait_ge(wf_step, 4)
                nc.vector.tensor_tensor(wf_up[:], wf_up[:], wf_down[:], ALU.subtract).then_inc(wf_step, 1)
                dve.wait_ge(wf_step, 5)
                nc.vector.tensor_tensor(wf_down[:], wf_up[:], wf[:], ALU.subtract).then_inc(wf_step, 1)
                dve.wait_ge(wf_step, 6)
                nc.vector.tensor_tensor(wf_up[:], wf[:], wf_down[:], ALU.add).then_inc(wf_ready, 1)

            def ternary_copy(_):
                dve.wait_ge(wft_ps, 1)
                nc.vector.tensor_copy(wf_t[:].rearrange("p c n -> p (c n)"), c_ps[:]).then_inc(y_made, 1)

            def rope_products(a, t):
                wait(dve, qk_ps, a.count(2, t + 1))
                wait(dve, rope_made[t], a.count(1, 0))
                src = a1_ps if t == 0 else a0_ps
                n = QK // HD
                nc.vector.tensor_tensor(rope_c[:, t].rearrange("p (n i) -> p n i", i=HD),
                                        src[:].rearrange("p (n i) -> p n i", i=HD),
                                        spread(tab[:, t, TAB_COS:TAB_SIN], 1, n), ALU.mult)
                for half in range(2):
                    other = 1 - half
                    last = nc.vector.tensor_tensor(
                        rope_s[:, t, half * D:(half + 1) * D].rearrange("p (n i) -> p n i", i=HD),
                        src[:, other * D:(other + 1) * D].rearrange("p (n i) -> p n i", i=HD),
                        spread(tab[:, t, TAB_SIN + half * HD:TAB_SIN + (half + 1) * HD], 1, n // 2), ALU.mult)
                last.then_inc(rope_mul, 1)

            def qkt_copy(a, n):
                wait(dve, qkt_ps, a.count(8, n + 1))
                wait(dve, scoret_done, a.count(FILLS, -FILLS))
                dst = (q_t if n < 4 else k_t)[a.slot]
                nc.vector.tensor_copy(dst[:, 2 * (n % 4):2 * (n % 4) + 2, :].rearrange("p u s -> p (u s)"),
                                      qkt_banks[n % 4][:]).then_inc(qkt_dve, 1)

            def maxima(a, m):
                for n in (2 * m, 2 * m + 1):
                    r, t, pairs, keys = score_fill(n)
                    wait(dve, score_done, a.count(FILLS, n + 1))
                    nc.vector.tensor_reduce(neg_max[:, t, r, pairs.start:pairs.stop],
                                            score_ps[r][:].rearrange("p (h k) -> p h k", k=keys),
                                            AX.X, ALU.max, negate=True).then_inc(max_done, 1)

            def split_maxima(b):
                view = neg_max[:].rearrange("p t r u -> p t (r u)")
                dst = max_parts
                wait(dve, max_done, b.count(FILLS, FILLS))
                wait(dve, maxt_ps, b.count(1, 0))
                nc.vector.tensor_copy(dst[:, :, 0], view).then_inc(maxh_made, 1)
                wait(dve, maxh_made, b.count(1, 1))
                nc.vector.tensor_tensor(dst[:, :, 1], view, dst[:, :, 0].bitcast(F32), ALU.subtract).then_inc(max_split, 1)

            def o_copy(b):
                wait(dve, pv_done, b.count(G, 2))
                nc.vector.tensor_copy(o_t[b.slot][:, 0, :], pv_ps[:]).then_inc(o_made[0], 1)

            def normalise_attention(c, t):
                wait(dve, ot_ps, c.count(2, t + 1))
                heads = ot_banks[t][:].rearrange("p (h n) -> p h n", h=H)
                nc.vector.reciprocal(rsum[:, t], heads[:, :, HD]).then_inc(rsum_made, 1)
                wait(dve, rsum_made, c.count(2, t + 1))
                nc.vector.tensor_tensor(attn[:, t], heads[:, :, 0:HD], spread(rsum[:, t], 2, HD),
                                        ALU.mult).then_inc(attn_made, 1)

            def first_statistics(z):
                if isinstance(z.pair, int) and z.c < 2:
                    dve.wait_ge(x_in[z.c], 16)
                else:
                    dve.wait_ge(x_in[2], 16 * (B - 2))
                    dve.wait_ge(memsets, 9)
                statistics(z, stats, mean_var, x_tiles(z), stats_step, var_made)

            def first_normalise(z):
                wait(dve, rstd_made, z.count(1, 1))
                wait(dve, xnt_ps, z.count(1, 0))
                normalise(xn, x_tiles(z), mean_var, rstd, xn_made)

            def xn_low(a):
                wait(dve, xnh_made, a.count(1, 1))
                wait(dve, v_ps, a.count(1, 0))
                nc.vector.tensor_tensor(xn_l[:].rearrange("p c s -> p (c s)"), a0_ps[:],
                                        xn_h[:].bitcast(F32).rearrange("p c s -> p (c s)"),
                                        ALU.subtract).then_inc(xnl_made, 1)

            def residual(c):
                wait(dve, proj_ps, c.count(1, 1))
                wait(dve, x_bias_made, c.count(1, 1))
                nc.vector.tensor_tensor(x2[:].rearrange("p t d -> p (t d)"), c_ps[:],
                                        x_bias[:].rearrange("p t d -> p (t d)"),
                                        ALU.add).then_inc(x2_made, 1)
                wait(dve, x2_made, c.count(1, 1))
                statistics(c, stats2, mean_var2, [x2[:, t] for t in range(T)], stats2_step, var2_made)

            def second_normalise(c):
                wait(dve, rstd2_made, c.count(1, 1))
                normalise(xn2, [x2[:, t] for t in range(T)], mean_var2, rstd2, xn2_made)

            def output(c):
                wait(dve, ffn_ps, c.count(1, 1))
                wait(dve, x2_bias_made, c.count(1, 1))
                nc.vector.tensor_tensor(xs[:, c.number()].rearrange("p t d -> p (t d)"), c_ps[:],
                                        x2_bias[:].rearrange("p t d -> p (t d)"), ALU.add).then_inc(y_made, 1)

            def turn(z, a, b, c):
                do(z, first_statistics)
                do(a, xn_low)
                do(b, maxima, 0)
                do(b, maxima, 1)
                do(first(z), ternary_sum)
                do(c, o_copy)
                do(b, maxima, 2)
                do(first(a), bias_parts)
                do(b, maxima, 3)
                do(b, maxima, 4)
                do(first(a), ternary_weights)
                do(a, rope_products, 0)
                do(c, normalise_attention, 0)
                do(c, normalise_attention, 1)
                do(b, maxima, 5)
                do(b, split_maxima)
                do(first(a), masks)
                do(a, rope_products, 1)
                do(a, rope_sum, dve, 1)
                do(first(a), low_value_weights)
                do(first(a), ternary_copy)
                do(a, low_parts, dve, 1)
                do(c, residual)
                do(first(z), low_weights, 0)
                do(a, qkt_copy, 1)
                do(z, first_normalise)
                do(c, second_normalise)
                do(a, qkt_copy, 5)
                do(first(z), low_weights, 1)
                do(c, output)

            turns(dve, turn)

        @block.tensor
        def _(pe):
            mm = nc.tensor.matmul

            def transposed(dst, src, sig, value=1):
                for c in range(C):
                    for t in range(T):
                        last = nc.tensor.transpose(dst[:, c * S + t * P:c * S + (t + 1) * P],
                                                   src[:, t, c * P:(c + 1) * P], ident)
                last.then_inc(sig, value)

            def ternary_scale(_):
                pe.wait_ge(wf_step, 1)
                pe.wait_ge(memsets, 9)
                mm(c_ps[:, 0:1], ones[:], wf_abs[:, 0:1], start=True, stop=True).then_inc(wf_sum_ps, 1)

            def ternary_transpose(_):
                pe.wait_ge(wf_ready, 1)
                transposed(c_ps, wf_up, wft_ps)

            def project(a, dst, wh, wl, cols, bias_from, t, sig):
                n = cols.stop - cols.start
                mm(dst[:, cols], ones_r[:], bias_rows[:, bias_from:bias_from + n], start=True, stop=False)
                for c in range(C):
                    toks = slice(t * P, (t + 1) * P)
                    for xpart, wpart in ((xn_h, wh), (xn_h, wl), (xn_l, wh)):
                        last = mm(dst[:, cols], xpart[:, c, toks], wpart[:, c, :], start=False,
                                  stop=c == C - 1 and xpart is xn_l)
                if sig is not None:
                    last.then_inc(sig, 1)

            def xn_transpose(a):
                wait(pe, xn_made, a.count(1, 1))
                wait_qkt_of_last(pe, a, 4)
                transposed(a0_ps, xn, xnt_ps)

            def qk_project(a, t):
                if t == 0:
                    if first(a):
                        pe.wait_ge(bias_made, 6)
                        pe.wait_ge(wl_made, 4)
                        pe.wait_ge(memsets, 9)
                    wait(pe, xnh_made, a.count(1, 1))
                    wait(pe, xnl_made, a.count(1, 1))
                    wait_qkt_of_last(pe, a, 5)
                project(a, a1_ps if t == 0 else a0_ps, wqk_h, wqk_l, slice(0, QK), 0, t, qk_ps)

            def v_project(a):
                wait(pe, rope_mul, a.count(2, 1))
                if first(a):
                    pe.wait_ge(wvl_made, 2)
                project(a, a1_ps, wv_h, wv_l, slice(0, D), QK, 0, None)
                project(a, a1_ps, wv_h, wv_l, slice(D, 2 * D), QK, 1, v_ps)

            def qk_transpose(a, n):
                if n == 0:
                    wait(pe, low_made[0], a.count(1, 1))
                    wait(pe, low_made[1], a.count(1, 1))
                    if first(a):
                        pe.wait_ge(masks_made, 3)
                    wait(pe, rope_mul, a.count(2, 2))
                if n == 1:
                    wait(pe, v_made, a.count(1, 1))
                if n == 2 and a.c > 0:
                    wait(pe, max_done, a.count(FILLS, 0))
                if n >= 4:
                    wait_qkt_evacuated(pe, a, n - 4)
                for i in range(2):
                    u = 2 * (n % 4) + i
                    for t in range(T):
                        parts = (q_parts if n < 4 else k_parts)[:, t, 2 * u:2 * u + 2, :]
                        last = nc.tensor.transpose(qkt_banks[n % 4][:, i * S + t * P:i * S + (t + 1) * P].bitcast(F32R),
                                                   parts.rearrange("p h n -> p (h n)"), ident_r[:])
                last.then_inc(qkt_ps, 1)

            def scores(a, m):
                if m == 0:
                    wait_qkt_evacuated(pe, a, 7)
                    wait_qkt_evacuated(pe, a, 5)
                for n in (2 * m, 2 * m + 1):
                    r, t, pairs, keys = score_fill(n)
                    wait(pe, max_done, a.count(FILLS, n - 1))
                    dst = score_ps[r]
                    diagonal = dst[:].rearrange("p (h k) -> p h k", k=keys)[:, :, keys - P:keys]
                    mm(diagonal, ident_bf[:], mask_bf[:, 0:len(pairs), :], start=True, stop=False,
                       skip_group_check=True)
                    rows = slice(ROWS * r, ROWS * r + PROD)
                    for i, u in enumerate(pairs):
                        last = mm(dst[:, i * keys:(i + 1) * keys], q_t[a.slot][rows, u, t * P:(t + 1) * P],
                                  k_t[a.slot][rows, u, 0:keys], start=False, stop=u == pairs[-1],
                                  skip_group_check=True)
                    last.then_inc(score_done, 1)

            def maxima_transpose(b):
                wait(pe, max_split, b.count(1, 1))
                if b.c > 0:
                    wait(pe, attn_made, b.count(2, 0))
                for t in range(T):
                    last = nc.tensor.transpose(pv_ps[0:2 * H, t * P:(t + 1) * P],
                                               max_parts[:, t].bitcast(F32).rearrange("p w h -> p (w h)"), ident)
                last.then_inc(maxt_ps, 1)

            def scores_t(b, m):
                if m == 0:
                    wait(pe, max_rows[b.slot], b.slot_count(64, 64))
                for n in (2 * m, 2 * m + 1):
                    wait(pe, exp_done, b.count(FILLS, n - 1))
                    r, t, pairs = scoret_fill(n)
                    width = S - t * P
                    rows = slice(ROWS * r, ROWS * (r + 1))
                    for i, u in enumerate(pairs):
                        last = mm(scoret_ps[r][:, i * width:(i + 1) * width],
                                  k_t[b.slot][rows, u, t * P:(t + 1) * P],
                                  q_t[b.slot][rows, u, t * P:S], start=True, stop=True)
                    last.then_inc(scoret_done, 1)

            def values(b, g):
                wait(pe, causal_done, b.count(FILLS, GROUP_FILLS[g]))
                wait(pe, v_made, b.count(1, 1))
                if g == 0:
                    wait(pe, maxt_made, b.count(1, 1))
                if g == 2:
                    wait(pe, o_made[0], b.count(1, 1))
                pr, e = probs[g // 2], g % 2
                base = (g % 2) * S
                for t in range(T):
                    for i in range(4):
                        u, r = i // 2, i % 2
                        if t == 0:
                            src = pr[:, 4 * e + r, u * S:(u + 1) * S]
                        else:
                            src = pr[:, 2 + r, (2 * e + u) * P:(2 * e + u + 1) * P]
                        last = mm(pv_ps[VW * i:VW * (i + 1), base + t * P:base + S], v[b.slot][:, t, 4 * g + i, :],
                                  src, start=t == 0, stop=t == 1)
                last.then_inc(pv_done, 1)

            def o_transpose(c):
                wait(pe, o_made[0], c.count(1, 1))
                wait(pe, o_made[1], c.count(1, 1))
                wait(pe, y_made, c.count(1, 1))
                for t in range(T):
                    for g in range(G):
                        last = nc.tensor.transpose(
                            ot_banks[t][:, g * P:(g + 1) * P],
                            o_t[c.slot][:, g // 2, (g % 2) * S + t * P:(g % 2) * S + (t + 1) * P], ident)
                    last.then_inc(ot_ps, 1)

            def linear(src_t, w, sig):
                for t in range(T):
                    cols = slice(t * D, (t + 1) * D)
                    for c in range(C):
                        last = mm(c_ps[:, cols], src_t[:, c, t * P:(t + 1) * P], w[:, c, :], start=c == 0,
                                  stop=c == C - 1)
                last.then_inc(sig, 1)

            pe.wait_ge(consts_in, 16)

            def attn_transpose(c):
                wait(pe, attn_made, c.count(2, 2))
                transposed(c_ps, attn[:].rearrange("p t h d -> p t (h d)"), attnt_ps)

            def attn_project(c):
                wait(pe, attnt_made, c.count(1, 1))
                linear(attn_t, wo, proj_ps)

            def xn2_transpose(c):
                wait(pe, xn2_made, c.count(1, 1))
                transposed(c_ps, xn2, xn2t_ps)

            def ternary_linear(c):
                wait(pe, xn2t_made, c.count(1, 1))
                linear(xn2_t, wf_t, ffn_ps)

            def turn(z, a, b, c):
                do(b, scores, 0)
                do(first(z), ternary_scale)
                do(c, scores_t, 3)
                do(c, values, 0)
                do(c, scores_t, 4)
                do(b, scores, 1)
                do(c, values, 1)
                do(c, scores_t, 5)
                do(b, scores, 2)
                do(c, values, 2)
                do(b, scores, 3)
                do(c, values, 3)
                do(b, scores, 4)
                do(a, qk_project, 0)
                do(c, o_transpose)
                do(b, scores, 5)
                do(a, qk_project, 1)
                do(first(a), ternary_transpose)
                do(c, attn_transpose)
                do(b, maxima_transpose)
                do(a, v_project)
                do(c, attn_project)
                do(a, qk_transpose, 0)
                do(a, qk_transpose, 1)
                do(a, qk_transpose, 2)
                do(a, qk_transpose, 3)
                do(b, scores_t, 0)
                do(a, qk_transpose, 4)
                do(a, qk_transpose, 5)
                do(a, qk_transpose, 6)
                do(b, scores_t, 1)
                do(c, xn2_transpose)
                do(a, qk_transpose, 7)
                do(z, xn_transpose)
                do(b, scores_t, 2)
                do(c, ternary_linear)

            turns(pe, turn)


def constants():
    inv_freq = (np.float32(1.0) / np.float32(10000.0) ** (np.arange(0, HD, 2, dtype=np.float32) / np.float32(HD)))
    freq = np.arange(S, dtype=np.float32)[:, None] * inv_freq.astype(np.float32)[None, :]
    for_x, for_rotated = np.sin(freq), np.cos(freq)
    scale = np.float32(HD ** -0.5)
    table = np.zeros((P, C_END), np.float32)
    for t in range(T):
        rows = slice(t * P, (t + 1) * P)
        at = C_TAB + t * TAB
        table[:, at:at + HD] = np.concatenate([for_x[rows] * scale, for_x[rows]], 1)
        rotated = np.concatenate([for_rotated[rows] * scale, for_rotated[rows]], 1)
        table[:, at + HD:at + 2 * HD] = -rotated
        table[:, at + 2 * HD:at + 3 * HD] = rotated
    table[:, C_ID:C_MASK] = np.eye(P, dtype=np.float32)
    table[:, C_MASK:C_SEL] = np.where(np.arange(P)[None, :] > np.arange(P)[:, None], np.float32(MASKED), np.float32(0))
    table[0, C_SEL] = 1.0
    table[1, C_SEL + 1] = 1.0
    return table


_INS = ["L0_attn_x", "L0_attn_w_qkv", "L0_attn_b_qkv", "L0_attn_w_o", "L0_attn_b_o", "L0_ffn_weight", "L0_ffn_bias"]


def kernel(**inputs):
    import concourse.bacc as bacc
    from concourse.bass_utils import run_bass_kernel_spmd

    nc = bacc.Bacc("TRN2", target_bir_lowering=False, num_devices=1)
    arrays = {f"in_{name}": np.ascontiguousarray(inputs[name]) for name in _INS}
    arrays["in_consts"] = constants()
    args = [nc.dram_tensor(name, a.shape, mybir.dt.from_np(a.dtype), kind="ExternalInput").ap()
            for name, a in arrays.items()]
    args.append(nc.dram_tensor("out_y", (B, S, D), F32, kind="ExternalOutput").ap())
    layer_kernel(nc, *args)
    r = run_bass_kernel_spmd(nc, [arrays], core_ids=[0])
    return r.results[0]["out_y"]
```

```python
from contextlib import ExitStack

import numpy as np

import concourse.bass as bass
from concourse import mybir

F32 = mybir.dt.float32
F32R = mybir.dt.float32r
BF16 = mybir.dt.bfloat16
ALU = mybir.AluOpType
ACT = mybir.ActivationFunctionType
AX = mybir.AxisListType

P = 128
B, S, D = 8, 256, 256
H, HD = 16, 16
T = S // P
C = D // P
HALF = HD // 2
QK = 2 * D
ROWS = 64
PROD = 3 * HD
PAIRS = H // 2
G = H // 4
VW = 32
FILLS = 3 * G
BIAS_LOW = 32
EPS = 1e-5
TERNARY_EPS = 1e-10
MASKED = -9e15
TAB_COS, TAB_SIN = 0, HD
TAB = HD + 2 * HD
C_TAB, C_ID, C_MASK, C_END = 0, T * TAB, T * TAB + P, T * TAB + 2 * P


def do(seq, step, *args):
    if seq:
        step(seq, *args)


def first(seq):
    return seq if seq and isinstance(seq.pair, int) and seq.c == 0 else None


def final(seq):
    return seq if seq and isinstance(seq.pair, int) and seq.c == B - 1 else None


class Seq:

    def __init__(self, c, pair=0):
        self.c, self.pair, self.slot = c, pair, c % 2

    def number(self):
        return self.pair * 2 + self.c

    def count(self, per, n):
        least = per * self.c + n
        if isinstance(self.pair, int):
            return least
        assert least > 0
        return self.pair * (2 * per) + least

    def slot_count(self, per, n):
        least = per * (self.c // 2) + n
        if isinstance(self.pair, int):
            return least
        assert least > 0
        return self.pair * per + least


def wait(eng, sem, value):
    if not isinstance(value, int) or value > 0:
        eng.wait_ge(sem, value)


def wait_apart(eng, sem, value, passed):
    wait(eng, sem, value)
    if not isinstance(value, int):
        eng.sem_inc(passed, 1)


def spread(ap, axis, n):
    ap = ap.unsqueeze(axis)
    shape = list(ap.shape)
    shape[axis] = n
    return ap.to_broadcast(shape)


def layer_kernel(nc, x, w_qkv, b_qkv, w_o, b_o, w_f, b_f, consts, out):
    ctx = ExitStack()
    with ctx:
        def sb(name, shape, dt=F32):
            return ctx.enter_context(nc.sbuf_tensor(name, shape, dt))

        def sem(name):
            return ctx.enter_context(nc.semaphore(name))

        const = sb("const", [P, C_END])
        tab = const[:, C_TAB:C_ID].rearrange("p (t n) -> p t n", t=T)
        ident = const[:, C_ID:C_MASK]
        ident_bf = sb("ident_bf", [P, P], BF16)
        ident_r = sb("ident_r", [P, P], F32R)
        mask_bf = sb("mask_bf", [P, 4, P], BF16)
        wqkv = sb("wqkv", [P, C, 3 * D])
        wqk_h = sb("wqk_h", [P, C, QK], F32R)
        wqk_l = sb("wqk_l", [P, C, QK], F32R)
        wv_h = sb("wv_h", [P, C, D], F32R)
        wv_l = sb("wv_l", [P, C, D], F32R)
        wo = sb("wo", [P, C, D])
        wf = sb("wf", [P, C, D])
        wf_up = sb("wf_up", [P, C, D])
        wf_down = sb("wf_down", [P, C, D])
        wf_t = sb("wf_t", [P, C, D])
        wf_abs = sb("wf_abs", [P, 2])
        wf_scale = sb("wf_scale", [P, 4])
        ones = sb("ones", [P, P])
        zeros_bf = sb("zeros_bf", [P, 512], BF16)
        bias = sb("bias", [BIAS_LOW + 1, 3 * D])
        bias_h = sb("bias_h", [BIAS_LOW + 1, QK], F32R)
        bias_rows = sb("bias_rows", [BIAS_LOW + 1, QK], F32R)
        linear_bias = sb("linear_bias", [P, 2, D])
        qkv_bias = sb("qkv_bias", [P, 3 * D])
        ones_r = sb("ones_r", [BIAS_LOW + 1, P], F32R)
        xs = sb("xs", [P, B + 1, T, D])
        stats = sb("stats", [P, T, 6])
        mean_var = sb("mean_var", [P, T, 2])
        rstd = sb("rstd", [P, 2, T])
        minus_half = sb("minus_half", [P, T])
        xn = sb("xn", [P, T, D])
        xn_h = sb("xn_h", [P, C, S], F32R)
        xn_l = sb("xn_l", [P, C, S], F32R)
        rope_c = sb("rope_c", [P, T, QK])
        rope_s = sb("rope_s", [P, T, QK])
        roped = sb("roped", [P, T, H, 2, HD])
        q_parts = sb("q_parts", [P, T, H, ROWS], F32R)
        k_parts = sb("k_parts", [P, T, H, ROWS], F32R)
        q_t = [sb(f"q_t{i}", [P, PAIRS, S], F32R) for i in range(2)]
        k_t = [sb(f"k_t{i}", [P, PAIRS, S], F32R) for i in range(2)]
        v = [sb(f"v{i}", [P, T, H, VW]) for i in range(2)]
        neg_max = sb("neg_max", [P, T, 2, PAIRS])
        max_parts = sb("max_parts", [P, T, 2, 2, PAIRS], F32R)
        max_t = sb("max_t", [2 * H, S])
        probs = [sb(f"probs{i}", [P, FILLS // 2, 512]) for i in range(2)]
        o_t = [sb(f"o_t{i}", [P, 2, 512]) for i in range(2)]
        rsum = sb("rsum", [P, T, H])
        attn = sb("attn", [P, T, H, HD])
        attn_t = sb("attn_t", [P, C, S])
        x_bias = sb("x_bias", [P, T, D])
        x2 = sb("x2", [P, T, D])
        x2_bias = sb("x2_bias", [P, T, D])
        stats2 = sb("stats2", [P, T, 6])
        mean_var2 = sb("mean_var2", [P, T, 2])
        rstd2 = sb("rstd2", [P, 2, T])
        xn2 = sb("xn2", [P, T, D])
        xn2_t = sb("xn2_t", [P, C, S])

        def bank(name):
            return ctx.enter_context(nc.psum_tensor(name, [P, 512], F32))

        score_ps = [bank(f"score_ps{i}") for i in range(2)]
        scoret_ps = [bank(f"scoret_ps{i}") for i in range(2)]
        pv_ps = bank("pv_ps")
        a0_ps = bank("a0_ps")
        a1_ps = bank("a1_ps")
        c_ps = bank("c_ps")

        consts_in, w_in = sem("consts_in"), sem("w_in")
        wqkv_in = [sem(f"wqkv_in{c}") for c in range(C)]
        bias_in, v_bias_in, linear_bias_in = sem("bias_in"), sem("v_bias_in"), sem("linear_bias_in")
        x_in = [sem(f"x_in{i}") for i in range(3)]
        memsets = sem("memsets")
        zeros_made = sem("zeros_made")
        dve_passed, pool_passed = sem("dve_passed"), sem("pool_passed")
        masks_made = sem("masks_made")
        wh_made, wl_made = sem("wh_made"), sem("wl_made")
        wvh_made, wvl_made = sem("wvh_made"), sem("wvl_made")
        bias_h_made, bias_made = sem("bias_h_made"), sem("bias_made")
        wf_step, wf_sum_ps, wf_ready, wft_ps = (
            sem(n) for n in ("wf_step", "wf_sum_ps", "wf_ready", "wft_ps"))
        stats_step = sem("stats_step")
        var_made = sem("var_made")
        rstd_step, rstd_made = sem("rstd_step"), sem("rstd_made")
        xn_made = sem("xn_made")
        xnt_ps = sem("xnt_ps")
        xnh_made, xnl_made = sem("xnh_made"), sem("xnl_made")
        qk_ps, v_ps = sem("qk_ps"), sem("v_ps")
        rope_mul = sem("rope_mul")
        rope_made = [sem(f"rope_made{t}") for t in range(T)]
        high_made = sem("high_made")
        low_made = [sem(f"low_made{t}") for t in range(T)]
        v_made = sem("v_made")
        qkt_ps = sem("qkt_ps")
        qkt_act, qkt_dve = sem("qkt_act"), sem("qkt_dve")
        score_done = sem("score_done")
        max_done = sem("max_done")
        maxh_made, max_split = sem("maxh_made"), sem("max_split")
        maxt_ps, maxt_made = sem("maxt_ps"), sem("maxt_made")
        max_rows = [sem(f"max_rows{i}") for i in range(2)]
        scoret_done = sem("scoret_done")
        exp_done = sem("exp_done")
        causal_done = sem("causal_done")
        pv_done = sem("pv_done")
        o_made = [sem(f"o_made{i}") for i in range(2)]
        ot_ps = sem("ot_ps")
        rsum_made, attn_made = sem("rsum_made"), sem("attn_made")
        attnt_ps, attnt_made = sem("attnt_ps"), sem("attnt_made")
        x_bias_made, x2_bias_made = sem("x_bias_made"), sem("x2_bias_made")
        proj_ps, x2_made = sem("proj_ps"), sem("x2_made")
        stats2_step, var2_made = sem("stats2_step"), sem("var2_made")
        rstd2_step, rstd2_made = sem("rstd2_step"), sem("rstd2_made")
        xn2_made, xn2t_ps, xn2t_made = sem("xn2_made"), sem("xn2t_ps"), sem("xn2t_made")
        ffn_ps = sem("ffn_ps")
        y_made = sem("y_made")
        y_out = sem("y_out")

        LOOPS = (B - 2) // 2

        def turns(eng, turn):
            turn(Seq(0), None, None, None)
            turn(Seq(1), Seq(0), None, None)
            turn(Seq(2), Seq(1), Seq(0), None)
            with eng.Fori(0, LOOPS) as pair:
                for u in range(2):
                    turn(Seq(3 + u, pair), Seq(2 + u, pair), Seq(1 + u, pair), Seq(u, pair))
            turn(None, None, Seq(B - 1), Seq(B - 2))
            turn(None, None, None, Seq(B - 1))

        def score_fill(n):
            r, m = n % 2, n // 2
            return (r, 0, range(4 * m, 4 * m + 4), P) if m < 2 else (r, 1, range(2 * m - 4, 2 * m - 2), S)

        def scoret_fill(n):
            r, octet, m = n % 2, n // (FILLS // 2), n % (FILLS // 2) // 2
            first = 4 * octet
            return r, m % 2, (range(first, first + 2), range(first, first + 4), range(first + 2, first + 4))[m]

        GROUP_FILLS = (4, 6, 10, FILLS)

        qkt_banks = [a0_ps, a1_ps, *score_ps]
        QKT_ACT = (0, 1, 2, 3, 4, 6, 7)
        QKT_DVE = (5,)

        ot_banks = [c_ps, pv_ps]

        def wait_qkt_evacuated(eng, s, n):
            copied, mine = (qkt_act, QKT_ACT) if n in QKT_ACT else (qkt_dve, QKT_DVE)
            wait(eng, copied, s.count(len(mine), mine.index(n) + 1))

        def wait_qkt_of_last(eng, s, n):
            copied, mine = (qkt_act, QKT_ACT) if n in QKT_ACT else (qkt_dve, QKT_DVE)
            wait(eng, copied, s.count(len(mine), mine.index(n) + 1 - len(mine)))

        def rope_sum(a, eng, t):
            wait(eng, rope_mul, a.count(2, t + 1))
            wait(eng, low_made[t], a.count(1, 0))
            for half in range(2):
                dst = roped[:, t, :, :, half * HALF:(half + 1) * HALF].rearrange("p h w i -> p (h w) i")
                cos = rope_c[:, t, half * D:(half + 1) * D].rearrange("p (n i) -> p n i", i=HALF)
                sin = rope_s[:, t, half * D:(half + 1) * D].rearrange("p (n i) -> p n i", i=HALF)
                last = eng.tensor_tensor(dst, cos, sin, ALU.add)
            last.then_inc(rope_made[t], 1)

        def low_parts(a, eng, t):
            wait(eng, high_made, a.count(2, t + 1))
            eng.tensor_tensor(q_parts[:, t, :, HD:2 * HD], roped[:, t, :, 0, :],
                              q_parts[:, t, :, 0:HD].bitcast(F32), ALU.subtract)
            eng.tensor_tensor(k_parts[:, t, :, 2 * HD:PROD], roped[:, t, :, 1, :],
                              k_parts[:, t, :, 0:HD].bitcast(F32), ALU.subtract).then_inc(low_made[t], 1)

        block = ctx.enter_context(nc.Block())

        @block.sync
        def _(sp):
            sp.dma_start(xs[:, 0], x[0].rearrange("(t p) d -> p t d", p=P)).then_inc(x_in[0], 16)
            sp.dma_start(const[:], consts).then_inc(consts_in, 16)
            sp.dma_start(bias[:], b_qkv.rearrange("(a n) -> a n", a=1).to_broadcast([BIAS_LOW + 1, 3 * D])).then_inc(bias_in, 16)
            sp.dma_start(qkv_bias[:], b_qkv.rearrange("(a n) -> a n", a=1).to_broadcast([P, 3 * D])).then_inc(v_bias_in, 16)
            sp.dma_start(xs[:, 1], x[1].rearrange("(t p) d -> p t d", p=P)).then_inc(x_in[1], 16)
            sp.dma_start(wo[:], w_o.rearrange("(c p) n -> p c n", p=P)).then_inc(w_in, 16)
            sp.dma_start(wf[:], w_f.rearrange("(c p) n -> p c n", p=P)).then_inc(w_in, 16)
            for i, b in enumerate((b_o, b_f)):
                sp.dma_start(linear_bias[:, i, :],
                             b.rearrange("(a n) -> a n", a=1).to_broadcast([P, D])).then_inc(linear_bias_in, 16)
            for n in range(2, B):
                sp.dma_start(xs[:, n], x[n].rearrange("(t p) d -> p t d", p=P)).then_inc(x_in[2], 16)

            def move_maxima(b):
                wait(sp, maxt_made, b.count(1, 1))
                for r in range(2):
                    row = ROWS * r + PROD
                    sp.dma_start(q_t[b.slot][row:row + 2, :, :].bitcast(F32),
                                 max_t[r * H:(r + 1) * H, :]
                                 ).then_inc(max_rows[b.slot], 16)

            def store(c):
                wait(sp, y_made, c.count(1, 2))
                sp.dma_start(out[c.number()].rearrange("(t p) d -> p t d", p=P),
                             xs[:, c.number()]).then_inc(y_out, 16)

            def turn(z, a, b, c):
                do(b, move_maxima)
                do(c, store)

            turns(sp, turn)
            sp.wait_ge(y_out, 16 * B)

        @block.gpsimd
        def _(pool):
            nc.gpsimd.memset(zeros_bf[:], 0.0).then_inc(zeros_made, 1)
            nc.gpsimd.memset(bias_rows[:].bitcast(F32), 0.0).then_inc(memsets, 1)
            nc.gpsimd.memset(minus_half[:], -0.5).then_inc(memsets, 1)

            def fill_constants(_):
                nc.gpsimd.memset(xs[:, B], 0.0).then_inc(memsets, 1)
                nc.gpsimd.memset(ones[:], 1.0).then_inc(memsets, 1)
                nc.gpsimd.memset(ones_r[:].bitcast(F32), 1.0).then_inc(memsets, 1)
                for i in range(2):
                    nc.gpsimd.memset(v[i][:, :, :, HD:VW], 1.0).then_inc(memsets, 1)
                nc.gpsimd.memset(q_parts[:, :, :, PROD:ROWS].bitcast(F32), 0.0).then_inc(memsets, 1)
                nc.gpsimd.memset(k_parts[:, :, :, PROD:PROD + 2].bitcast(F32), 1.0).then_inc(memsets, 1)
                nc.gpsimd.memset(k_parts[:, :, :, PROD + 2:ROWS].bitcast(F32), 0.0).then_inc(memsets, 1)

            def inverse_deviation(dst, mv, var_sem, step_sem, made_sem, s):
                wait_apart(pool, var_sem, s.count(1, 1), pool_passed)
                nc.gpsimd.tensor_scalar(dst[:, 0], mv[:, :, 1], 1.0, EPS, ALU.mult, ALU.add).then_inc(step_sem, 1)
                wait(pool, step_sem, s.count(1, 1))
                nc.gpsimd.tensor_tensor(dst[:, 1], dst[:, 0], minus_half[:], ALU.pow).then_inc(made_sem, 1)

            def causal(b, m):
                for n in (2 * m, 2 * m + 1):
                    wait_apart(pool, exp_done, b.count(FILLS, n + 1), pool_passed)
                    _, _, pairs = scoret_fill(n)
                    blk = probs[n // 6][:, n % 6, :].rearrange("p (h q) -> p h q", h=len(pairs))[:, :, 0:P]
                    nc.gpsimd.affine_select(out=blk, in_=blk, compare_op=ALU.is_ge, fill=0.0, base=0,
                                            pattern=[[0, blk.shape[1]], [1, P]],
                                            channel_multiplier=-1).then_inc(causal_done, 1)

            def add_bias(c):
                if first(c):
                    pool.wait_ge(linear_bias_in, 32)
                nc.gpsimd.tensor_tensor(x_bias[:], xs[:, c.number()], spread(linear_bias[:, 0], 1, T),
                                        ALU.add).then_inc(x_bias_made, 1)

            def add_bias2(c):
                wait(pool, x2_made, c.count(1, 1))
                nc.gpsimd.tensor_tensor(x2_bias[:], x2[:], spread(linear_bias[:, 1], 1, T),
                                        ALU.add).then_inc(x2_bias_made, 1)

            def deviation(z):
                inverse_deviation(rstd, mean_var, var_made, rstd_step, rstd_made, z)

            def deviation2(c):
                inverse_deviation(rstd2, mean_var2, var2_made, rstd2_step, rstd2_made, c)

            def turn(z, a, b, c):
                do(c, causal, 3)
                do(c, causal, 4)
                do(a, low_parts, pool, 0)
                do(c, causal, 5)
                do(z, deviation)
                do(c, deviation2)
                do(b, causal, 0)
                do(c, add_bias2)
                do(b, causal, 1)
                do(b, causal, 2)
                do(b, add_bias)
                do(first(z), fill_constants)
                do(z, rope_sum, pool, 0)

            turns(pool, turn)

        @block.scalar
        def _(act):
            for c in range(C):
                act.dma_start(wqkv[:, c, :], w_qkv[c * P:(c + 1) * P, :]).then_inc(wqkv_in[c], 16)

            def high_weights(_, c):
                act.wait_ge(wqkv_in[c], 16)
                w = wqkv[:, c, :].rearrange("p (h w s i) -> p h w s i", h=H, w=3, s=2)
                for s in range(2):
                    dst = wqk_h[:, c, s * D:(s + 1) * D].rearrange("p (h w i) -> p h w i", h=H, w=2)
                    nc.scalar.copy(dst, w[:, :, 0:2, s, :]).then_inc(wh_made, 1)

            def high_value_weights(_):
                for c in range(C):
                    nc.scalar.copy(wv_h[:, c, :].rearrange("p (h d) -> p h d", h=H),
                                   wqkv[:, c, :].rearrange("p (h n) -> p h n", h=H)[:, :, 2 * HD:]).then_inc(wvh_made, 1)

            def high_bias(_):
                act.wait_ge(bias_in, 16)
                act.wait_ge(memsets, 1)
                for row, dst in ((0, bias_rows), (BIAS_LOW, bias_h)):
                    src = bias[row:row + 1, :].rearrange("p (h w s i) -> p h w s i", h=H, w=3, s=2)
                    for s in range(2):
                        nc.scalar.copy(dst[row:row + 1, s * D:(s + 1) * D].rearrange("p (h w i) -> p h w i", h=H, w=2),
                                       src[:, :, 0:2, s, :]).then_inc(bias_h_made, 1)

            def max_t_copy(b):
                wait(act, maxt_ps, b.count(1, 1))
                if b.c >= 1 or not isinstance(b.pair, int):
                    before = Seq(b.c - 1, b.pair)
                    wait(act, max_rows[before.slot], before.slot_count(32, 32))
                nc.scalar.copy(max_t[:], pv_ps[0:2 * H, 0:S]).then_inc(maxt_made, 1)

            def high_parts(a, t):
                wait(act, rope_made[t], a.count(1, 1))
                wait(act, qkt_ps, a.count(8, 0))
                nc.scalar.copy(q_parts[:, t].rearrange("p h (r d) -> p h r d", r=4)[:, :, 0:3:2, :],
                               spread(roped[:, t, :, 0, :], 2, 2))
                nc.scalar.copy(k_parts[:, t, :, 0:2 * HD].rearrange("p h (r d) -> p h r d", r=2),
                               spread(roped[:, t, :, 1, :], 2, 2)).then_inc(high_made, 1)

            def qkt_copy(a, n):
                wait(act, qkt_ps, a.count(8, n + 1))
                wait(act, scoret_done, a.count(FILLS, -FILLS))
                dst = (q_t if n < 4 else k_t)[a.slot]
                nc.scalar.copy(dst[:, 2 * (n % 4):2 * (n % 4) + 2, :].rearrange("p u s -> p (u s)"),
                               qkt_banks[n % 4][:]).then_inc(qkt_act, 1)

            def exps(b, m):
                if m % 3 == 0:
                    wait(act, pv_done, b.count(G, 2 * (m // 3) - 2))
                for n in (2 * m, 2 * m + 1):
                    wait(act, scoret_done, b.count(FILLS, n + 1))
                    nc.scalar.activation(probs[n // 6][:, n % 6, :], scoret_ps[n % 2][:], ACT.Exp).then_inc(exp_done, 1)

            def xn_high(a):
                wait(act, xnt_ps, a.count(1, 1))
                wait(act, v_ps, a.count(1, 0))
                nc.scalar.copy(xn_h[:].rearrange("p c s -> p (c s)"), a0_ps[:]).then_inc(xnh_made, 1)

            def attn_t_copy(c):
                wait(act, attnt_ps, c.count(1, 1))
                nc.scalar.copy(attn_t[:].rearrange("p c s -> p (c s)"), c_ps[:]).then_inc(attnt_made, 1)

            def xn2_t_copy(c):
                wait(act, xn2t_ps, c.count(1, 1))
                nc.scalar.copy(xn2_t[:].rearrange("p c s -> p (c s)"), c_ps[:]).then_inc(xn2t_made, 1)

            def o_copy(c, octet):
                wait(act, pv_done, c.count(G, 2 * octet + 2))
                nc.scalar.copy(o_t[c.slot][:, octet, :], pv_ps[:]).then_inc(o_made[octet], 1)

            def turn(z, a, b, c):
                do(c, exps, 4)
                do(first(a), high_value_weights)
                do(a, high_parts, 0)
                do(c, o_copy, 0)
                do(c, exps, 5)
                do(a, high_parts, 1)
                do(c, o_copy, 1)
                do(a, qkt_copy, 0)
                do(first(z), high_weights, 0)
                do(first(z), high_bias)
                do(first(z), high_weights, 1)
                do(b, max_t_copy)
                do(c, attn_t_copy)
                do(a, qkt_copy, 1)
                do(a, qkt_copy, 2)
                do(a, qkt_copy, 3)
                do(a, qkt_copy, 4)
                do(a, qkt_copy, 6)
                do(a, qkt_copy, 7)
                do(z, xn_high)
                do(b, exps, 0)
                do(b, exps, 1)
                do(b, exps, 2)
                do(b, exps, 3)
                do(c, xn2_t_copy)

            turns(act, turn)

        @block.vector
        def _(dve):
            def normalise(dst, src, mv, rs, made):
                for t in range(T):
                    last = nc.vector.tensor_scalar(dst[:, t], src[t], mv[:, t, 0:1], rs[:, 1, t:t + 1],
                                                   ALU.subtract, ALU.mult)
                last.then_inc(made, 1)

            def statistics(s, st, mv, src, step, made):
                for t in range(T):
                    nc.vector.bn_stats(st[:, t], src[t]).then_inc(step, 1)
                for t in range(T):
                    wait_apart(dve, step, s.count(T, t + 1), dve_passed)
                    last = nc.vector.bn_aggr(mv[:, t], st[:, t])
                last.then_inc(made, 1)

            def x_tiles(a):
                return [xs[:, a.number(), t, :] for t in range(T)]

            def low_weights(_, c):
                w = wqkv[:, c, :].rearrange("p (h w s i) -> p h w s i", h=H, w=3, s=2)
                for s in range(2):
                    dve.wait_ge(wh_made, 2 * c + s + 1)
                    view = dict(h=H, w=2)
                    nc.vector.tensor_tensor(
                        wqk_l[:, c, s * D:(s + 1) * D].rearrange("p (h w i) -> p h w i", **view),
                        w[:, :, 0:2, s, :],
                        wqk_h[:, c, s * D:(s + 1) * D].bitcast(F32).rearrange("p (h w i) -> p h w i", **view),
                        ALU.subtract).then_inc(wl_made, 1)

            def low_value_weights(_):
                for c in range(C):
                    dve.wait_ge(wvh_made, c + 1)
                    nc.vector.tensor_tensor(
                        wv_l[:, c, :].rearrange("p (h d) -> p h d", h=H),
                        wqkv[:, c, :].rearrange("p (h n) -> p h n", h=H)[:, :, 2 * HD:],
                        wv_h[:, c, :].bitcast(F32).rearrange("p (h d) -> p h d", h=H),
                        ALU.subtract).then_inc(wvl_made, 1)

            def low_bias(_):
                row = slice(BIAS_LOW, BIAS_LOW + 1)
                src = bias[row, :].rearrange("p (h w s i) -> p h w s i", h=H, w=3, s=2)
                dve.wait_ge(bias_h_made, 4)
                for s in range(2):
                    high, low = (z[row, s * D:(s + 1) * D].rearrange("p (h w i) -> p h w i", h=H, w=2)
                                 for z in (bias_h, bias_rows))
                    nc.vector.tensor_tensor(low, src[:, :, 0:2, s, :], high.bitcast(F32),
                                            ALU.subtract).then_inc(bias_made, 1)

            def masks(_):
                dve.wait_ge(consts_in, 16)
                nc.vector.tensor_copy(ident_bf[:], ident).then_inc(masks_made, 1)
                nc.vector.tensor_copy(ident_r[:], ident).then_inc(masks_made, 1)
                nc.vector.tensor_copy(mask_bf[:], spread(const[:, C_MASK:C_END], 1, 4)).then_inc(masks_made, 1)

            def ternary_sum(_):
                dve.wait_ge(w_in, 32)
                nc.vector.tensor_reduce(wf_abs[:, 0:1], wf[:], AX.XY, ALU.add,
                                        apply_absolute_value=True).then_inc(wf_step, 1)

            def ternary_weights(_):
                dve.wait_ge(wf_sum_ps, 1)
                nc.vector.tensor_scalar(wf_scale[:, 0:1], c_ps[:, 0:1], 1.0 / (D * D), None, ALU.mult).then_inc(wf_step, 1)
                dve.wait_ge(wf_step, 2)
                nc.vector.tensor_scalar(wf_scale[:, 1:2], wf_scale[:, 0:1], TERNARY_EPS, 0.5, ALU.add, ALU.mult)
                nc.vector.tensor_scalar(wf_scale[:, 2:3], wf_scale[:, 0:1], TERNARY_EPS, -0.5, ALU.add,
                                        ALU.mult).then_inc(wf_step, 1)
                dve.wait_ge(wf_step, 3)
                nc.vector.tensor_scalar(wf_up[:], wf[:], wf_scale[:, 1:2], wf_scale[:, 0:1], ALU.is_gt, ALU.mult)
                nc.vector.tensor_scalar(wf_down[:], wf[:], wf_scale[:, 2:3], wf_scale[:, 0:1], ALU.is_lt,
                                        ALU.mult).then_inc(wf_step, 1)
                dve.wait_ge(wf_step, 4)
                nc.vector.tensor_tensor(wf_up[:], wf_up[:], wf_down[:], ALU.subtract).then_inc(wf_step, 1)
                dve.wait_ge(wf_step, 5)
                nc.vector.tensor_tensor(wf_down[:], wf_up[:], wf[:], ALU.subtract).then_inc(wf_step, 1)
                dve.wait_ge(wf_step, 6)
                nc.vector.tensor_tensor(wf_up[:], wf[:], wf_down[:], ALU.add).then_inc(wf_ready, 1)

            def ternary_copy(_):
                dve.wait_ge(wft_ps, 1)
                nc.vector.tensor_copy(wf_t[:].rearrange("p c n -> p (c n)"), c_ps[:]).then_inc(y_made, 1)

            def rope_products(a, t):
                wait(dve, qk_ps, a.count(2, t + 1))
                wait(dve, rope_made[t], a.count(1, 0))
                src = a1_ps if t == 0 else a0_ps
                n = QK // HD
                nc.vector.tensor_tensor(rope_c[:, t].rearrange("p (n i) -> p n i", i=HD),
                                        src[:].rearrange("p (n i) -> p n i", i=HD),
                                        spread(tab[:, t, TAB_COS:TAB_SIN], 1, n), ALU.mult)
                for half in range(2):
                    other = 1 - half
                    last = nc.vector.tensor_tensor(
                        rope_s[:, t, half * D:(half + 1) * D].rearrange("p (n i) -> p n i", i=HD),
                        src[:, other * D:(other + 1) * D].rearrange("p (n i) -> p n i", i=HD),
                        spread(tab[:, t, TAB_SIN + half * HD:TAB_SIN + (half + 1) * HD], 1, n // 2), ALU.mult)
                last.then_inc(rope_mul, 1)

            def v_copy(a):
                wait(dve, v_ps, a.count(1, 1))
                wait(dve, pv_done, a.count(G, -G))
                if first(a):
                    dve.wait_ge(v_bias_in, 16)
                v_bias = qkv_bias[:].rearrange("p (h n) -> p h n", h=H)[:, :, 2 * HD:]
                nc.vector.tensor_tensor(v[a.slot][:, :, :, 0:HD],
                                        a1_ps[:].rearrange("p (t h d) -> p t h d", t=T, h=H),
                                        spread(v_bias, 1, T), ALU.add).then_inc(v_made, 1)

            def qkt_copy(a, n):
                wait(dve, qkt_ps, a.count(8, n + 1))
                wait(dve, scoret_done, a.count(FILLS, -FILLS))
                dst = (q_t if n < 4 else k_t)[a.slot]
                nc.vector.tensor_copy(dst[:, 2 * (n % 4):2 * (n % 4) + 2, :].rearrange("p u s -> p (u s)"),
                                      qkt_banks[n % 4][:]).then_inc(qkt_dve, 1)

            def maxima(a, m):
                for n in (2 * m, 2 * m + 1):
                    r, t, pairs, keys = score_fill(n)
                    wait(dve, score_done, a.count(FILLS, n + 1))
                    nc.vector.tensor_reduce(neg_max[:, t, r, pairs.start:pairs.stop],
                                            score_ps[r][:].rearrange("p (h k) -> p h k", k=keys),
                                            AX.X, ALU.max, negate=True).then_inc(max_done, 1)

            def split_maxima(b):
                view, dst = neg_max[:], max_parts
                wait(dve, max_done, b.count(FILLS, FILLS))
                wait(dve, maxt_ps, b.count(1, 0))
                nc.vector.tensor_copy(dst[:, :, :, 0], view).then_inc(maxh_made, 1)
                wait(dve, maxh_made, b.count(1, 1))
                nc.vector.tensor_tensor(dst[:, :, :, 1], view, dst[:, :, :, 0].bitcast(F32), ALU.subtract).then_inc(max_split, 1)

            def normalise_attention(c, t):
                wait(dve, ot_ps, c.count(2, t + 1))
                heads = ot_banks[t][:].rearrange("p (h n) -> p h n", h=H)
                nc.vector.reciprocal(rsum[:, t], heads[:, :, HD]).then_inc(rsum_made, 1)
                wait(dve, rsum_made, c.count(2, t + 1))
                nc.vector.tensor_tensor(attn[:, t], heads[:, :, 0:HD], spread(rsum[:, t], 2, HD),
                                        ALU.mult).then_inc(attn_made, 1)

            def first_statistics(z):
                if isinstance(z.pair, int) and z.c < 2:
                    dve.wait_ge(x_in[z.c], 16)
                else:
                    dve.wait_ge(x_in[2], 16 * (B - 2))
                    dve.wait_ge(memsets, 10)
                statistics(z, stats, mean_var, x_tiles(z), stats_step, var_made)

            def first_normalise(z):
                wait(dve, rstd_made, z.count(1, 1))
                wait(dve, xnt_ps, z.count(1, 0))
                normalise(xn, x_tiles(z), mean_var, rstd, xn_made)

            def xn_low(a):
                wait(dve, xnh_made, a.count(1, 1))
                wait(dve, v_ps, a.count(1, 0))
                nc.vector.tensor_tensor(xn_l[:].rearrange("p c s -> p (c s)"), a0_ps[:],
                                        xn_h[:].bitcast(F32).rearrange("p c s -> p (c s)"),
                                        ALU.subtract).then_inc(xnl_made, 1)

            def residual(c):
                wait(dve, proj_ps, c.count(1, 1))
                wait(dve, x_bias_made, c.count(1, 1))
                nc.vector.tensor_tensor(x2[:].rearrange("p t d -> p (t d)"), c_ps[:],
                                        x_bias[:].rearrange("p t d -> p (t d)"),
                                        ALU.add).then_inc(x2_made, 1)
                wait(dve, x2_made, c.count(1, 1))
                statistics(c, stats2, mean_var2, [x2[:, t] for t in range(T)], stats2_step, var2_made)

            def second_normalise(c):
                wait(dve, rstd2_made, c.count(1, 1))
                normalise(xn2, [x2[:, t] for t in range(T)], mean_var2, rstd2, xn2_made)

            def output(c):
                wait(dve, ffn_ps, c.count(1, 1))
                wait(dve, x2_bias_made, c.count(1, 1))
                nc.vector.tensor_tensor(xs[:, c.number()].rearrange("p t d -> p (t d)"), c_ps[:],
                                        x2_bias[:].rearrange("p t d -> p (t d)"), ALU.add).then_inc(y_made, 1)

            def turn(z, a, b, c):
                do(a, low_parts, dve, 1)
                do(b, maxima, 5)
                do(c, normalise_attention, 0)
                do(b, split_maxima)
                do(c, normalise_attention, 1)
                do(a, v_copy)
                do(z, first_statistics)
                do(z, first_normalise)
                do(first(z), low_weights, 0)
                do(a, qkt_copy, 5)
                do(c, residual)
                do(first(z), masks)
                do(first(z), low_weights, 1)
                do(first(z), low_bias)
                do(z, xn_low)
                do(c, second_normalise)
                do(a, maxima, 0)
                do(first(b), ternary_weights)
                do(z, rope_products, 0)
                do(a, maxima, 1)
                do(z, rope_products, 1)
                do(a, maxima, 2)
                do(z, rope_sum, dve, 1)
                do(a, maxima, 3)
                do(first(b), ternary_copy)
                do(c, output)
                do(a, maxima, 4)
                do(first(z), low_value_weights)
                do(first(z), ternary_sum)

            turns(dve, turn)

        @block.tensor
        def _(pe):
            mm = nc.tensor.matmul

            def transposed(dst, src, sig, value=1):
                for c in range(C):
                    for t in range(T):
                        last = nc.tensor.transpose(dst[:, c * S + t * P:c * S + (t + 1) * P],
                                                   src[:, t, c * P:(c + 1) * P], ident)
                last.then_inc(sig, value)

            def busy_start(_, n):
                if n == 0:
                    pe.wait_ge(zeros_made, 1)
                for _ in range(2):
                    mm(c_ps[:], zeros_bf[:, 0:P], zeros_bf[:], start=True, stop=True)

            def busy_end(s, n):
                if n == 0:
                    pe.wait_ge(max_done, FILLS * B)
                for _ in range(4):
                    mm(score_ps[0][:], zeros_bf[:, 0:P], zeros_bf[:], start=True, stop=True)

            def ternary_scale(_):
                pe.wait_ge(wf_step, 1)
                pe.wait_ge(memsets, 10)
                mm(c_ps[:, 0:1], ones[:], wf_abs[:, 0:1], start=True, stop=True).then_inc(wf_sum_ps, 1)

            def ternary_transpose(_):
                pe.wait_ge(wf_ready, 1)
                transposed(c_ps, wf_up, wft_ps)

            def project(dst, wh, wl, t, start):
                toks = slice(t * P, (t + 1) * P)
                for c in range(C):
                    for xpart, wpart in ((xn_h, wh), (xn_h, wl), (xn_l, wh)):
                        last = mm(dst, xpart[:, c, toks], wpart[:, c, :], start=start, stop=c == C - 1 and xpart is xn_l)
                        start = False
                return last

            def xn_transpose(a):
                wait(pe, xn_made, a.count(1, 1))
                if first(a):
                    pe.wait_ge(consts_in, 16)
                wait_qkt_of_last(pe, a, 4)
                transposed(a0_ps, xn, xnt_ps)

            def qk_project(a, t):
                if t == 0:
                    if first(a):
                        pe.wait_ge(bias_made, 2)
                        pe.wait_ge(wl_made, 4)
                        pe.wait_ge(memsets, 10)
                    wait(pe, xnh_made, a.count(1, 1))
                    wait(pe, xnl_made, a.count(1, 1))
                    wait_qkt_of_last(pe, a, 5)
                dst = (a1_ps if t == 0 else a0_ps)[:]
                mm(dst, ones_r[:], bias_rows[:], start=True, stop=False)
                project(dst, wqk_h, wqk_l, t, start=False).then_inc(qk_ps, 1)

            def v_project(a):
                wait(pe, rope_mul, a.count(2, 1))
                if first(a):
                    pe.wait_ge(wvl_made, 2)
                for t in range(T):
                    last = project(a1_ps[:, t * D:(t + 1) * D], wv_h, wv_l, t, start=True)
                last.then_inc(v_ps, 1)

            def qk_transpose(a, n):
                if n == 0:
                    wait(pe, low_made[0], a.count(1, 1))
                    wait(pe, low_made[1], a.count(1, 1))
                    if first(a):
                        pe.wait_ge(masks_made, 3)
                    wait(pe, rope_mul, a.count(2, 2))
                if n == 1:
                    wait(pe, v_made, a.count(1, 1))
                if n == 2 and a.c > 0:
                    wait(pe, max_done, a.count(FILLS, 0))
                if n >= 4:
                    wait_qkt_evacuated(pe, a, n - 4)
                for i in range(2):
                    u = 2 * (n % 4) + i
                    for t in range(T):
                        parts = (q_parts if n < 4 else k_parts)[:, t, 2 * u:2 * u + 2, :]
                        dst = qkt_banks[n % 4][:, i * S + t * P:i * S + (t + 1) * P]
                        last = nc.tensor.transpose(dst.bitcast(F32R), parts.rearrange("p h n -> p (h n)"), ident_r[:])
                last.then_inc(qkt_ps, 1)

            def scores(a, m):
                if m == 0:
                    wait_qkt_evacuated(pe, a, 7)
                    wait_qkt_evacuated(pe, a, 5)
                for n in (2 * m, 2 * m + 1):
                    r, t, pairs, keys = score_fill(n)
                    wait(pe, max_done, a.count(FILLS, n - 1))
                    dst = score_ps[r]
                    diagonal = dst[:].rearrange("p (h k) -> p h k", k=keys)[:, :, keys - P:keys]
                    mm(diagonal, ident_bf[:], mask_bf[:, 0:len(pairs), :], start=True, stop=False,
                       skip_group_check=True)
                    rows = slice(ROWS * r, ROWS * r + PROD)
                    for i, u in enumerate(pairs):
                        last = mm(dst[:, i * keys:(i + 1) * keys], q_t[a.slot][rows, u, t * P:(t + 1) * P],
                                  k_t[a.slot][rows, u, 0:keys], start=False, stop=u == pairs[-1],
                                  skip_group_check=True)
                    last.then_inc(score_done, 1)

            def maxima_transpose(b):
                wait(pe, max_split, b.count(1, 1))
                if b.c > 0:
                    wait(pe, attn_made, b.count(2, 0))
                for t in range(T):
                    last = nc.tensor.transpose(pv_ps[0:2 * H, t * P:(t + 1) * P].bitcast(F32R),
                                               max_parts[:, t].rearrange("p r w u -> p (r w u)"), ident_r[:])
                last.then_inc(maxt_ps, 1)

            def scores_t(b, m):
                if m == 0:
                    wait(pe, max_rows[b.slot], b.slot_count(32, 32))
                for n in (2 * m, 2 * m + 1):
                    wait(pe, exp_done, b.count(FILLS, n - 1))
                    r, t, pairs = scoret_fill(n)
                    width = S - t * P
                    rows = slice(ROWS * r, ROWS * (r + 1))
                    for i, u in enumerate(pairs):
                        last = mm(scoret_ps[r][:, i * width:(i + 1) * width],
                                  k_t[b.slot][rows, u, t * P:(t + 1) * P],
                                  q_t[b.slot][rows, u, t * P:S], start=True, stop=True)
                    last.then_inc(scoret_done, 1)

            def values(b, g):
                wait(pe, causal_done, b.count(FILLS, GROUP_FILLS[g]))
                wait(pe, v_made, b.count(1, 1))
                if g == 0:
                    wait(pe, maxt_made, b.count(1, 1))
                if g == 2:
                    wait(pe, o_made[0], b.count(1, 1))
                pr, e = probs[g // 2], g % 2
                base = (g % 2) * S
                for t in range(T):
                    for i in range(4):
                        u, r = i // 2, i % 2
                        if t == 0:
                            src = pr[:, 4 * e + r, u * S:(u + 1) * S]
                        else:
                            src = pr[:, 2 + r, (2 * e + u) * P:(2 * e + u + 1) * P]
                        last = mm(pv_ps[VW * i:VW * (i + 1), base + t * P:base + S], v[b.slot][:, t, 4 * g + i, :],
                                  src, start=t == 0, stop=t == 1)
                last.then_inc(pv_done, 1)

            def o_transpose(c):
                wait(pe, o_made[0], c.count(1, 1))
                wait(pe, o_made[1], c.count(1, 1))
                wait(pe, y_made, c.count(1, 1))
                for t in range(T):
                    for g in range(G):
                        last = nc.tensor.transpose(
                            ot_banks[t][:, g * P:(g + 1) * P],
                            o_t[c.slot][:, g // 2, (g % 2) * S + t * P:(g % 2) * S + (t + 1) * P], ident)
                    last.then_inc(ot_ps, 1)

            def linear(src_t, w, sig):
                for t in range(T):
                    cols = slice(t * D, (t + 1) * D)
                    for c in range(C):
                        last = mm(c_ps[:, cols], src_t[:, c, t * P:(t + 1) * P], w[:, c, :], start=c == 0,
                                  stop=c == C - 1)
                last.then_inc(sig, 1)

            def attn_transpose(c):
                wait(pe, attn_made, c.count(2, 2))
                transposed(c_ps, attn[:].rearrange("p t h d -> p t (h d)"), attnt_ps)

            def attn_project(c):
                wait(pe, attnt_made, c.count(1, 1))
                linear(attn_t, wo, proj_ps)

            def xn2_transpose(c):
                wait(pe, xn2_made, c.count(1, 1))
                transposed(c_ps, xn2, xn2t_ps)

            def ternary_linear(c):
                wait(pe, xn2t_made, c.count(1, 1))
                linear(xn2_t, wf_t, ffn_ps)

            def turn(z, a, b, c):
                do(first(b), busy_start, 7)
                do(b, scores, 4)
                do(c, values, 2)
                do(c, values, 3)
                do(first(a), busy_start, 4)
                do(b, scores, 5)
                do(c, o_transpose)
                do(a, v_project)
                do(a, qk_transpose, 0)
                do(final(c), busy_end, 4)
                do(final(b), busy_end, 0)
                do(b, maxima_transpose)
                do(c, attn_transpose)
                do(a, qk_transpose, 1)
                do(final(c), busy_end, 5)
                do(a, qk_transpose, 2)
                do(final(b), busy_end, 1)
                do(a, qk_transpose, 3)
                do(a, qk_transpose, 4)
                do(c, attn_project)
                do(a, qk_transpose, 5)
                do(a, qk_transpose, 6)
                do(a, qk_transpose, 7)
                do(z, xn_transpose)
                do(final(b), busy_end, 2)
                do(b, scores_t, 0)
                do(a, scores, 0)
                do(first(b), ternary_scale)
                do(final(c), busy_end, 6)
                do(final(b), busy_end, 3)
                do(first(z), busy_start, 0)
                do(final(c), busy_end, 7)
                do(first(z), busy_start, 1)
                do(b, scores_t, 1)
                do(z, qk_project, 0)
                do(final(c), busy_end, 8)
                do(a, scores, 1)
                do(b, scores_t, 2)
                do(z, qk_project, 1)
                do(first(z), busy_start, 2)
                do(c, xn2_transpose)
                do(b, scores_t, 3)
                do(b, values, 0)
                do(a, scores, 2)
                do(b, scores_t, 4)
                do(final(c), busy_end, 9)
                do(first(a), busy_start, 5)
                do(b, values, 1)
                do(a, scores, 3)
                do(b, scores_t, 5)
                do(first(a), busy_start, 6)
                do(first(b), ternary_transpose)
                do(first(z), busy_start, 3)
                do(c, ternary_linear)

            turns(pe, turn)


def constants():
    inv_freq = (np.float32(1.0) / np.float32(10000.0) ** (np.arange(0, HD, 2, dtype=np.float32) / np.float32(HD)))
    freq = np.arange(S, dtype=np.float32)[:, None] * inv_freq.astype(np.float32)[None, :]
    for_x, for_rotated = np.sin(freq), np.cos(freq)
    scale = np.float32(HD ** -0.5)
    table = np.zeros((P, C_END), np.float32)
    for t in range(T):
        rows = slice(t * P, (t + 1) * P)
        at = C_TAB + t * TAB
        table[:, at:at + HD] = np.concatenate([for_x[rows] * scale, for_x[rows]], 1)
        rotated = np.concatenate([for_rotated[rows] * scale, for_rotated[rows]], 1)
        table[:, at + HD:at + 2 * HD] = -rotated
        table[:, at + 2 * HD:at + 3 * HD] = rotated
    table[:, C_ID:C_MASK] = np.eye(P, dtype=np.float32)
    table[:, C_MASK:C_END] = np.where(np.arange(P)[None, :] > np.arange(P)[:, None], np.float32(MASKED), np.float32(0))
    return table


_INS = ["L0_attn_x", "L0_attn_w_qkv", "L0_attn_b_qkv", "L0_attn_w_o", "L0_attn_b_o", "L0_ffn_weight", "L0_ffn_bias"]


def kernel(**inputs):
    import concourse.bacc as bacc
    from concourse.bass_utils import run_bass_kernel_spmd

    nc = bacc.Bacc("TRN2", target_bir_lowering=False, num_devices=1)
    arrays = {f"in_{name}": np.ascontiguousarray(inputs[name]) for name in _INS}
    arrays["in_consts"] = constants()
    args = [nc.dram_tensor(name, a.shape, mybir.dt.from_np(a.dtype), kind="ExternalInput").ap()
            for name, a in arrays.items()]
    args.append(nc.dram_tensor("out_y", (B, S, D), F32, kind="ExternalOutput").ap())
    layer_kernel(nc, *args)
    r = run_bass_kernel_spmd(nc, [arrays], core_ids=[0])
    return r.results[0]["out_y"]
```
